# Optimizing a Trainium2 kernel written in Bass

```python
import numpy as np
import jax
import jax.numpy as jnp

def _softmax(x, axis=-1):
    return jax.nn.softmax(x, axis=axis)

def _gelu(x):
    return jax.nn.gelu(x, approximate=True)

def _silu(x):
    return jax.nn.silu(x)

def _sigmoid(x):
    return jax.nn.sigmoid(x)

def _layernorm(x, axis=-1, eps=1e-05):
    m = jnp.mean(x, axis=axis, keepdims=True)
    v = jnp.var(x, axis=axis, keepdims=True)
    return (x - m) / jnp.sqrt(v + eps)

def _scatter_add(tgt, idx, src, axis=0):
    return tgt.at[idx].add(src)

def _segment_sum(src, seg, n):
    return jax.ops.segment_sum(src, seg, n)
kernel_name = 'mk_xattn_seq_d2_seqx_r4_45867a'

def setup_inputs(seed: int=0):
    np.random.seed(seed)
    _w = jnp.asarray

    def _rec_inputs():
        import jax
        import jax.numpy as jnp
        _rk = jax.random.key(seed)
        x = 7.22e-05 + 1 * jax.random.normal(jax.random.fold_in(_rk, 1), (32, 256, 256), jnp.float32)
        _lenS = 256 - jax.random.randint(jax.random.fold_in(_rk, 7), (32,), 0, max(1, 256 // 4) + 1, jnp.int32)
        _lenS2 = 77 - jax.random.randint(jax.random.fold_in(_rk, 8), (32,), 0, max(1, 77 // 4) + 1, jnp.int32)
        _ctx_1024P = jax.random.normal(jax.random.fold_in(_rk, 11), (32, 16, 256), jnp.float32)
        _ctx_1024c = jax.random.dirichlet(jax.random.fold_in(_rk, 511), 0.3 * jnp.ones((16,), jnp.float32), (32, 77))
        _ctx_1024t = jnp.einsum('bsk,bkd->bsd', _ctx_1024c, _ctx_1024P)
        _ctx_1024t = _ctx_1024t * jax.lax.rsqrt(jnp.mean(jnp.square(_ctx_1024t)) + 1e-12) * 0.953939
        ctx_1024 = -1.39393e-06 + 0.999914 * (_ctx_1024t + 0.3 * jax.random.normal(jax.random.fold_in(_rk, 611), (32, 77, 256), jnp.float32))
        _validS = jnp.arange(256)[None, :] < _lenS[:, None]
        _validS2 = jnp.arange(77)[None, :] < _lenS2[:, None]
        _causal = jnp.tril(jnp.ones((256, 256), dtype=bool))
        mask_BxS2_ik0 = jnp.where(jnp.broadcast_to(_validS2[:, :], (32, 77)), 0, 1).astype(jnp.int32)
        return (x, ctx_1024, mask_BxS2_ik0)
    x, ctx_1024, mask_BxS2_ik0 = _rec_inputs()

    def _L0_xattn_setup():
        import jax, jax.numpy as jnp
        import numpy as np
        B, S, SE, D, H = (8, 256, 128, 256, 16)
        HD = D // H
        NEG = -100000.0
        EPS = 1e-05

        def _split_heads(t):
            b, t_, _ = t.shape
            return t.reshape(b, t_, H, HD).transpose(0, 2, 1, 3)

        def _merge_heads(t):
            b, _, t_, _ = t.shape
            return t.transpose(0, 2, 1, 3).reshape(b, t_, D)

        def _ln(x, g, b):
            mu = jnp.mean(x, -1, keepdims=True)
            var = jnp.var(x, -1, keepdims=True)
            return (x - mu) * jax.lax.rsqrt(var + EPS) * g + b

        def _block(x, enc_hidden, enc_padding_mask, w_attn, b_attn, w_oproj, b_oproj, w_fc, b_fc, w_mproj, b_mproj, ln1_g, ln1_b, ln2_g, ln2_b):
            inv = 1.0 / jnp.sqrt(jnp.float32(HD))
            qkv = x @ w_attn + b_attn
            q, k, v = jnp.split(qkv, 3, axis=-1)
            q, k, v = (_split_heads(q), _split_heads(k), _split_heads(v))
            w = jnp.einsum('bhqd,bhkd->bhqk', q, k) * inv
            causal = jnp.tril(jnp.ones((S, S), jnp.float32))[None, None]
            w = w * causal + NEG * (1.0 - causal)
            w = jax.nn.softmax(w, axis=-1)
            a_self = _merge_heads(jnp.einsum('bhqk,bhkd->bhqd', w, v)) @ w_oproj + b_oproj
            kv = enc_hidden @ w_attn[:, D:] + b_attn[D:]
            ck, cv = jnp.split(kv, 2, axis=-1)
            ck, cv = (_split_heads(ck), _split_heads(cv))
            cw = jnp.einsum('bhqd,bhkd->bhqk', q, ck) * inv
            amask = enc_padding_mask.astype(jnp.float32) * NEG
            cw = cw + amask[:, None, None, :]
            cw = jax.nn.softmax(cw, axis=-1)
            a_cross = _merge_heads(jnp.einsum('bhqk,bhkd->bhqd', cw, cv)) @ w_oproj + b_oproj
            a = 0.5 * (a_self + a_cross)
            n = _ln(x + a, ln1_g, ln1_b)
            m = jax.nn.gelu(n @ w_fc + b_fc, approximate=True) @ w_mproj + b_mproj
            h = _ln(n + m, ln2_g, ln2_b)
            return h
        key = jax.random.key(seed)
        ks = jax.random.split(key, 8)
        s = 0.02
        return {'x': jax.random.normal(ks[0], (B, S, D), jnp.float32), 'enc_hidden': jax.random.normal(ks[1], (B, SE, D), jnp.float32), 'enc_padding_mask': jax.random.randint(ks[2], (B, SE), 0, 2, jnp.int32), 'w_attn': jax.random.normal(ks[3], (D, 3 * D), jnp.float32) * s, 'b_attn': jnp.zeros((3 * D,), jnp.float32), 'w_oproj': jax.random.normal(ks[4], (D, D), jnp.float32) * s, 'b_oproj': jnp.zeros((D,), jnp.float32), 'w_fc': jax.random.normal(ks[5], (D, 4 * D), jnp.float32) * s, 'b_fc': jnp.zeros((4 * D,), jnp.float32), 'w_mproj': jax.random.normal(ks[6], (4 * D, D), jnp.float32) * s, 'b_mproj': jnp.zeros((D,), jnp.float32), 'ln1_g': jnp.ones((D,), jnp.float32), 'ln1_b': jnp.zeros((D,), jnp.float32), 'ln2_g': jnp.ones((D,), jnp.float32), 'ln2_b': jnp.zeros((D,), jnp.float32)}
    _L0_xattn_all = _L0_xattn_setup()
    _L0_xattn_in = {k: v for k, v in _L0_xattn_all.items() if k in ('w_attn', 'b_attn', 'w_oproj', 'b_oproj', 'w_fc', 'b_fc', 'w_mproj', 'b_mproj', 'ln1_g', 'ln1_b', 'ln2_g', 'ln2_b')}
    del _L0_xattn_all

    def _L1_xattn_setup():
        import jax, jax.numpy as jnp
        import numpy as np
        EPS = 1e-08
        key = jax.random.key(seed)
        ks = jax.random.split(key, 7)
        B, S, D = (16, 512, 256)
        Q = jax.random.normal(ks[0], (B, S, D), dtype=jnp.float32)
        K = jax.random.normal(ks[1], (B, S, D), dtype=jnp.float32)
        V = jax.random.normal(ks[2], (B, S, D), dtype=jnp.float32)
        std = float(np.sqrt(2.0 / (D + D)))
        W1 = jax.random.normal(ks[3], (D, D), dtype=jnp.float32) * std
        b1 = jnp.zeros((D,), dtype=jnp.float32)
        W2 = jax.random.normal(ks[4], (D, D), dtype=jnp.float32) * std
        b2 = jnp.zeros((D,), dtype=jnp.float32)
        return {'Q': Q, 'K': K, 'V': V, 'W1': W1, 'b1': b1, 'W2': W2, 'b2': b2}
    _L1_xattn_all = _L1_xattn_setup()
    _L1_xattn_in = {k: v for k, v in _L1_xattn_all.items() if k in ('W1', 'b1', 'W2', 'b2')}
    del _L1_xattn_all
    return {'x': x, 'ctx_1024': ctx_1024, 'mask_BxS2_ik0': mask_BxS2_ik0, 'L0_xattn_w_attn': _L0_xattn_in['w_attn'], 'L0_xattn_b_attn': _L0_xattn_in['b_attn'], 'L0_xattn_w_oproj': _L0_xattn_in['w_oproj'], 'L0_xattn_b_oproj': _L0_xattn_in['b_oproj'], 'L0_xattn_w_fc': _L0_xattn_in['w_fc'], 'L0_xattn_b_fc': _L0_xattn_in['b_fc'], 'L0_xattn_w_mproj': _L0_xattn_in['w_mproj'], 'L0_xattn_b_mproj': _L0_xattn_in['b_mproj'], 'L0_xattn_ln1_g': _L0_xattn_in['ln1_g'], 'L0_xattn_ln1_b': _L0_xattn_in['ln1_b'], 'L0_xattn_ln2_g': _L0_xattn_in['ln2_g'], 'L0_xattn_ln2_b': _L0_xattn_in['ln2_b'], 'L1_xattn_W1': _L1_xattn_in['W1'], 'L1_xattn_b1': _L1_xattn_in['b1'], 'L1_xattn_W2': _L1_xattn_in['W2'], 'L1_xattn_b2': _L1_xattn_in['b2']}

def reference(x, ctx_1024, mask_BxS2_ik0, L0_xattn_w_attn, L0_xattn_b_attn, L0_xattn_w_oproj, L0_xattn_b_oproj, L0_xattn_w_fc, L0_xattn_b_fc, L0_xattn_w_mproj, L0_xattn_b_mproj, L0_xattn_ln1_g, L0_xattn_ln1_b, L0_xattn_ln2_g, L0_xattn_ln2_b, L1_xattn_W1, L1_xattn_b1, L1_xattn_W2, L1_xattn_b2):
    import jax
    import jax.numpy as jnp

    def _L0_xattn_ref(x, enc_hidden, enc_padding_mask, w_attn, b_attn, w_oproj, b_oproj, w_fc, b_fc, w_mproj, b_mproj, ln1_g, ln1_b, ln2_g, ln2_b):
        import jax, jax.numpy as jnp
        import numpy as np
        B, S, SE, D, H = (8, 256, 128, 256, 16)
        HD = D // H
        NEG = -100000.0
        EPS = 1e-05

        def _split_heads(t):
            b, t_, _ = t.shape
            return t.reshape(b, t_, H, HD).transpose(0, 2, 1, 3)

        def _merge_heads(t):
            b, _, t_, _ = t.shape
            return t.transpose(0, 2, 1, 3).reshape(b, t_, D)

        def _ln(x, g, b):
            mu = jnp.mean(x, -1, keepdims=True)
            var = jnp.var(x, -1, keepdims=True)
            return (x - mu) * jax.lax.rsqrt(var + EPS) * g + b

        def _block(x, enc_hidden, enc_padding_mask, w_attn, b_attn, w_oproj, b_oproj, w_fc, b_fc, w_mproj, b_mproj, ln1_g, ln1_b, ln2_g, ln2_b):
            inv = 1.0 / jnp.sqrt(jnp.float32(HD))
            qkv = x @ w_attn + b_attn
            q, k, v = jnp.split(qkv, 3, axis=-1)
            q, k, v = (_split_heads(q), _split_heads(k), _split_heads(v))
            w = jnp.einsum('bhqd,bhkd->bhqk', q, k) * inv
            causal = jnp.tril(jnp.ones((S, S), jnp.float32))[None, None]
            w = w * causal + NEG * (1.0 - causal)
            w = jax.nn.softmax(w, axis=-1)
            a_self = _merge_heads(jnp.einsum('bhqk,bhkd->bhqd', w, v)) @ w_oproj + b_oproj
            kv = enc_hidden @ w_attn[:, D:] + b_attn[D:]
            ck, cv = jnp.split(kv, 2, axis=-1)
            ck, cv = (_split_heads(ck), _split_heads(cv))
            cw = jnp.einsum('bhqd,bhkd->bhqk', q, ck) * inv
            amask = enc_padding_mask.astype(jnp.float32) * NEG
            cw = cw + amask[:, None, None, :]
            cw = jax.nn.softmax(cw, axis=-1)
            a_cross = _merge_heads(jnp.einsum('bhqk,bhkd->bhqd', cw, cv)) @ w_oproj + b_oproj
            a = 0.5 * (a_self + a_cross)
            n = _ln(x + a, ln1_g, ln1_b)
            m = jax.nn.gelu(n @ w_fc + b_fc, approximate=True) @ w_mproj + b_mproj
            h = _ln(n + m, ln2_g, ln2_b)
            return h
        return _block(x, enc_hidden, enc_padding_mask, w_attn, b_attn, w_oproj, b_oproj, w_fc, b_fc, w_mproj, b_mproj, ln1_g, ln1_b, ln2_g, ln2_b)

    def _L1_xattn_ref(Q, K, V, W1, b1, W2, b2):
        import jax, jax.numpy as jnp
        import numpy as np
        EPS = 1e-08
        D = Q.shape[-1]
        scale = jnp.sqrt(jnp.float32(max(1.0, D))) + EPS
        scores = jnp.einsum('bqd,bkd->bqk', Q, K) / scale
        attn = jax.nn.softmax(scores, axis=-1)
        V_att = jnp.einsum('bqk,bkd->bqd', attn, V)
        X = Q + V_att
        h = jax.nn.relu(X @ W1.T + b1)
        out = h @ W2.T + b2 + X
        return out
    x = _L0_xattn_ref(x, ctx_1024, mask_BxS2_ik0, L0_xattn_w_attn, L0_xattn_b_attn, L0_xattn_w_oproj, L0_xattn_b_oproj, L0_xattn_w_fc, L0_xattn_b_fc, L0_xattn_w_mproj, L0_xattn_b_mproj, L0_xattn_ln1_g, L0_xattn_ln1_b, L0_xattn_ln2_g, L0_xattn_ln2_b)
    x = _L1_xattn_ref(x, ctx_1024, ctx_1024, L1_xattn_W1, L1_xattn_b1, L1_xattn_W2, L1_xattn_b2)
    return x

_drawn_inputs = setup_inputs


def setup_inputs(seed=0):
    import zlib

    import numpy as np

    out = dict(_drawn_inputs(seed))
    spreads = {'L0_xattn_b_attn': (0.0, 0.1),
     'L0_xattn_b_oproj': (0.0, 0.1),
     'L0_xattn_b_fc': (0.0, 0.1),
     'L0_xattn_b_mproj': (0.0, 0.1),
     'L0_xattn_ln1_g': (1.0, 0.2),
     'L0_xattn_ln1_b': (0.0, 0.1),
     'L0_xattn_ln2_g': (1.0, 0.2),
     'L0_xattn_ln2_b': (0.0, 0.1),
     'L1_xattn_b1': (0.0, 0.1),
     'L1_xattn_b2': (0.0, 0.1)}
    factors = {}
    for name, (base, spread) in spreads.items():
        noise = np.random.default_rng([zlib.crc32(name.encode()), seed]).standard_normal(out[name].shape)
        drawn = base * np.exp(spread * noise) if base else spread * noise
        out[name] = jnp.asarray(drawn.astype(out[name].dtype))
    for name, factor in factors.items():
        out[name] = (out[name] * factor).astype(out[name].dtype)
    return out
```

```python
from contextlib import ExitStack

import numpy as np

import concourse.bass as bass
from concourse import mybir

ALU = mybir.AluOpType
ACT = mybir.ActivationFunctionType
F32 = mybir.dt.float32
BF16 = mybir.dt.bfloat16
F16 = mybir.dt.float16
I32 = mybir.dt.int32
AX_X = mybir.AxisListType.X

P = 128
B, S, D = 32, 256, 256
SE = 77
H, HD = 16, 16
F = 4 * D
KC = D // P
TB = S // P
FC = F // P
QH = 4
QUADS = H // QH
EPS = 1e-5
NEG = -100000.0

Q_PARTS = (0, 1, 2, 0, 1, 0)
K_PARTS = (0, 0, 0, 1, 1, 2)
SLOTS = len(Q_PARTS)
ROW_MASK = SLOTS * HD
ROW_SELF = ROW_MASK + 2
ROW_CROSS = ROW_SELF + 2
ROWS = ROW_CROSS + 2
COL_Q, COL_K, COL_C = 0, S, 2 * S
COLS = 2 * S + SE
GROUPS = 2
GH = H // GROUPS

SELF0, SELF1, CROSS = 0, QH * S, QH * S + QH * P
QUAD_COLS = CROSS + QH * S
HV = HD + 1
UNITS = TB * QH * 2
CROSS_RUN = 6
S_BANKS = 8 + 4 + 2 * 3
T_BANKS = 5 * QUADS
MAIN_READS = 9


class Seq:

    def __init__(self, n, half, par):
        self.n, self.half, self.par = n, half, par


def wait(eng, sem, value):
    if not (isinstance(value, int) and value <= 0):
        eng.wait_ge(sem, value)


def build(nc, x, xT, ctx_t, ctxT, mask, w_qk, b_qk, w_v, b_v, w_o, b_o, w_fc, b_fc, w_m, b_m,
          g1, be1, g2, be2, w1T, b1, w2T, b2, out):
    ctx = ExitStack()
    with ctx:
        def sb(name, shape, dt=F32):
            return ctx.enter_context(nc.sbuf_tensor(name, shape, dt))

        def bank(name):
            return ctx.enter_context(nc.psum_tensor(name, [P, 512], F32))

        def sem(name):
            return ctx.enter_context(nc.semaphore(name))

        parts_dram = nc.dram_tensor("parts_scratch", (3, P, GROUPS, COLS), BF16, kind="Internal").ap()
        mask_dram = nc.dram_tensor("mask_scratch", (B, 2, SE), BF16, kind="Internal").ap()

        wqk = sb("wqk", [P, KC, 2, GROUPS, P])
        bqk = sb("bqk", [P, 2, GROUPS])
        wv = sb("wv", [P, KC, D])
        wo = sb("wo", [P, KC, D])
        wfc = sb("wfc", [P, KC, F])
        bfc = sb("bfc", [P, FC])
        wm = sb("wm", [P, FC, D])
        w1s = sb("w1s", [P, KC, D])
        b1s = sb("b1s", [P, KC])
        w2s = sb("w2s", [P, KC, D])
        bv2, bo2, bm2, b22 = (sb(n, [P, TB, D]) for n in ("bv2", "bo2", "bm2", "b22"))
        g1s, be1s, g2s, be2s = (sb(n, [P, D]) for n in ("g1s", "be1s", "g2s", "be2s"))
        ident = sb("ident", [P, P])
        identb = sb("identb", [P, P], BF16)
        causal = sb("causal", [P, 4, P], BF16)
        half_pow = sb("half_pow", [P, TB])
        rows01 = sb("rows01", [1, 2, S], BF16)
        mask_i = sb("mask_i", [B, SE], I32)
        mask_f = sb("mask_f", [B, SE])
        mask_p = sb("mask_p", [B, 2, SE], BF16)
        ptick = sb("ptick", [P, 3])
        tick = sb("tick", [P, 4])

        xTs = [sb(f"xTs{p}", [P, KC, S]) for p in range(2)]
        cTs = [sb(f"cTs{p}", [P, KC, SE]) for p in range(2)]
        xt = [sb(f"xt{p}", [P, TB, D]) for p in range(2)]
        ct = [sb(f"ct{p}", [SE, D]) for p in range(2)]
        cTt = [sb(f"cTt{p}", [P, KC, SE]) for p in range(2)]
        stack = [sb(f"stack{p}", [ROWS, H, COLS], BF16) for p in range(2)]
        qk_f = sb("qk_f", [P, GROUPS, COLS])
        qk_r = sb("qk_r", [P, GROUPS, COLS])
        qk_p = sb("qk_p", [P, 3, GROUPS, COLS], BF16)
        v_f = sb("v_f", [P, 3, D])
        v_r = sb("v_r", [P, 3, D])
        v1 = [sb(f"v1_{p}", [P, 3, H, HV], BF16) for p in range(2)]
        v2 = [sb(f"v2_{p}", [P, 3, H, HD], BF16) for p in range(2)]
        v3 = [sb(f"v3_{p}", [P, 3, H, HD], BF16) for p in range(2)]
        mx = sb("mx", [P, TB, 2, H])
        mparts = sb("mparts", [P, TB, 2, 2, H], BF16)
        mT = sb("mT", [4 * H, S], BF16)
        pf = [sb(f"pf{p}", [P, QUAD_COLS]) for p in range(2)]
        ph = [sb(f"ph{p}", [P, QUAD_COLS], F16) for p in range(2)]
        pl = [sb(f"pl{p}", [P, QUAD_COLS], F16) for p in range(2)]
        rden = sb("rden", [P, UNITS])
        onorm = sb("onorm", [P, UNITS, HD])
        att = sb("att", [P, TB, H, HD])
        attT = sb("attT", [P, KC, S])
        xb = sb("xb", [P, TB, D])
        y = sb("y", [P, TB, D])
        stats = sb("stats", [P, TB, 6])
        mv = sb("mv", [P, TB, 2])
        ve = sb("ve", [P, TB])
        rstd = sb("rstd", [P, TB])
        scaled = sb("scaled", [P, TB, D])
        n1 = sb("n1", [P, TB, D])
        nT = sb("nT", [P, KC, S])
        nb = sb("nb", [P, TB, D])
        hid = sb("hid", [P, FC, S])
        z = y
        h1 = sb("h1", [P, TB, D])
        hT = sb("hT", [P, KC, S])
        nm = sb("nm", [P, TB])
        nms = sb("nms", [P, TB])
        p2 = sb("p2", [P, TB, SE])
        den2 = sb("den2", [P, TB])
        rden2 = sb("rden2", [P, TB])
        p2T = sb("p2T", [SE, S])
        x2 = sb("x2", [P, TB, D])
        x2T = sb("x2T", [P, KC, S])
        x2b = n1
        r2T = sb("r2T", [P, KC, S])
        o_sb = sb("o_sb", [P, TB, D])

        tb = [bank("t_bank0"), bank("t_bank1")]
        sbk = [bank("s_bank0"), bank("s_bank1")]
        ob = bank("o_bank")
        ga = bank("ga_bank")
        gc = [bank("gc_bank0"), bank("gc_bank1")]

        w_in = sem("w_in")
        const_pool = sem("const_pool")
        const_dve = sem("const_dve")
        const_dma = sem("const_dma")
        mask_in = sem("mask_in")
        x_in = [sem("x_in0"), sem("x_in1")]
        tok_in = [sem("tok_in0"), sem("tok_in1")]
        stack_in = [sem("stack_in0"), sem("stack_in1")]
        max_in = [sem("max_in0"), sem("max_in1")]
        parts_out = sem("parts_out")
        out_done = [sem("out_done0"), sem("out_done1")]
        qk_ready = sem("qk_ready")
        qk_evac = sem("qk_evac")
        qk_hi, qk_rest, qk_mid, qk_low = (sem(n) for n in ("qk_hi", "qk_rest", "qk_mid", "qk_low"))
        v_ready = sem("v_ready")
        v_evac = sem("v_evac")
        v_hi, v_rest, v_mid, v_low = (sem(n) for n in ("v_hi", "v_rest", "v_mid", "v_low"))
        s_ready = sem("s_ready")
        s_done = sem("s_done")
        m_hi = sem("m_hi")
        m_low = sem("m_low")
        mt_ready = sem("mt_ready")
        mt_evac = sem("mt_evac")
        t_ready = sem("t_ready")
        t_done = sem("t_done")
        causal_done = sem("causal_done")
        p_hi = sem("p_hi")
        pl_self = sem("pl_self")
        pl_cross = sem("pl_cross")
        pv_ready = sem("pv_ready")
        rden_ready = sem("rden_ready")
        pv_evac = sem("pv_evac")
        att_ready = sem("att_ready")
        gc0_ready = sem("gc0_ready")
        gc0_evac = sem("gc0_evac")
        gc1_ready = sem("gc1_ready")
        gc1_evac = sem("gc1_evac")
        xb_ready = sem("xb_ready")
        stat_ready = sem("stat_ready")
        mv_ready = sem("mv_ready")
        ve_ready = sem("ve_ready")
        rstd_ready = sem("rstd_ready")
        scaled_ready = sem("scaled_ready")
        n_ready = sem("n_ready")
        h_ready = sem("h_ready")
        nb_ready = sem("nb_ready")
        gelu_done = sem("gelu_done")
        relu_half = sem("relu_half")
        mask_float = sem("mask_float")
        nm_raw = sem("nm_raw")
        nm_ready = sem("nm_ready")
        p2_ready = sem("p2_ready")
        rden2_ready = sem("rden2_ready")
        x2_ready = sem("x2_ready")
        x2b_ready = sem("x2b_ready")
        o_ready = sem("o_ready")

        block = ctx.enter_context(nc.Block())

        def run(eng, body):
            def python_body(i):
                body(i, lambda n: Seq(n, n // 2, n % 2) if 0 <= n < B else None)

            for i in range(-2, 2):
                python_body(i)
            with eng.Fori(0, (B - 4) // 2) as j:
                for u in range(2):
                    body(None, lambda k, u=u: Seq(2 * j + (2 + u + k), j + (2 + u + k) // 2, (u + k) % 2))
            for i in range(B - 2, B + 1):
                python_body(i)

        def seqs(i, at):
            return [at(k if i is None else i + k) for k in (-1, 0, 1, 2)]

        @block.sync
        def _(sp):
            def load_x(s):
                sp.dma_start(xTs[s.par][:, :, :], xT[s.n]).then_inc(x_in[s.par], 16)
                sp.dma_start(cTs[s.par][:, :, :], ctxT[s.n]).then_inc(x_in[s.par], 16)

            sp.dma_start(mask_i[:, :], mask[:, :]).then_inc(mask_in, 16)
            sp.dma_start(xTs[0][:, :, :], xT[0]).then_inc(x_in[0], 16)
            sp.dma_start(cTs[0][:, :, :], ctxT[0]).then_inc(x_in[0], 16)
            loads = [(wqk[:, :, :, :, :], w_qk), (bqk[:, :, :], b_qk), (wv[:, :, :], w_v)]
            loads += [(t[:, b, :], v.partition_broadcast(P)) for t, v in ((bv2, b_v), (bo2, b_o), (bm2, b_m), (b22, b2))
                      for b in range(TB)]
            loads += [(wo[:, :, :], w_o), (wfc[:, :, :], w_fc), (bfc[:, :], b_fc), (wm[:, :, :], w_m),
                      (w1s[:, :, :], w1T), (b1s[:, :], b1), (w2s[:, :, :], w2T)]
            loads += [(t[:, :], v.partition_broadcast(P)) for t, v in ((g1s, g1), (be1s, be1), (g2s, g2), (be2s, be2))]
            for dst, src in loads:
                sp.dma_start(dst, src).then_inc(w_in, 16)
            assert len(loads) == N_LOADS
            load_x(Seq(1, 0, 1))
            sp.wait_ge(const_dve, 3)
            for p in range(2):
                for row, (q, k, c) in ((ROW_MASK, (1, 0, None)), (ROW_MASK + 1, (1, 0, None)),
                                       (ROW_SELF, (None, 1, 0)), (ROW_SELF + 1, (None, 1, 0)),
                                       (ROW_CROSS, (None, 0, 1)), (ROW_CROSS + 1, (None, 0, 1))):
                    for col, width, v in ((COL_Q, S, q), (COL_K, S, k), (COL_C, SE, c)):
                        if v is not None:
                            sp.dma_start(stack[p][row:row + 1, :, col:col + width],
                                         rows01[0:1, v, 0:width].rearrange("p (o c) -> p o c", o=1)
                                         .broadcast_to([1, H, width])).then_inc(const_dma, 16)
            sp.dma_start(mask_dram[:, :, :], mask_p[:, :, :]).then_inc(const_dma, 16)
            sp.wait_ge(const_dma, 16 * N_CONST_DMA)

            def stack_reads(s):
                wait(sp, t_ready, T_BANKS * (s.n - 1))
                st = stack[s.par]
                sp.dma_start(st[ROW_MASK:ROW_MASK + 2, :, COL_C:COLS],
                             mask_dram[s.n].rearrange("r (o c) -> r o c", o=1).broadcast_to([2, H, SE])
                             ).then_inc(stack_in[s.par], 16)
                sp.wait_ge(parts_out, 16 * (s.n + 1))
                src = parts_dram.rearrange("a (d h) g c -> (a d) (h g) c", d=HD)
                done = 0
                for rows, parts in ((0, 3), (3, 2), (5, 1)):
                    sp.dma_start(st[rows * HD:(rows + parts) * HD, :, COL_Q:COL_Q + S],
                                 src[0:parts * HD, :, COL_Q:COL_Q + S]).then_inc(stack_in[s.par], 16)
                    done += 1
                for slot, part in enumerate(K_PARTS):
                    sp.dma_start(st[slot * HD:(slot + 1) * HD, :, COL_K:COLS],
                                 src[part * HD:(part + 1) * HD, :, COL_K:COLS]).then_inc(stack_in[s.par], 16)
                    done += 1
                assert done == MAIN_READS

            def body(i, at):
                s_tail, s_att, s_next, s_qk = seqs(i, at)
                if s_qk and (i is None or s_qk.n >= 2):
                    sp.wait_ge(v_ready, 2 * (s_qk.n - 1))
                    load_x(s_qk)
                if s_next:
                    stack_reads(s_next)
                if s_att:
                    s = s_att
                    wait(sp, gc1_ready, 5 * (s.n - 1))
                    wait(sp, xb_ready, s.n - 1)
                    sp.dma_start(xt[s.par][:, :, :], x[s.n]).then_inc(tok_in[s.par], 16)
                    sp.dma_start(ct[s.par][:, :], ctx_t[s.n]).then_inc(tok_in[s.par], 16)
                    sp.dma_start(cTt[s.par][:, :, :], ctxT[s.n]).then_inc(tok_in[s.par], 16)
                if s_qk:
                    s = s_qk
                    sp.wait_ge(qk_hi, s.n + 1)
                    sp.wait_ge(qk_mid, s.n + 1)
                    sp.wait_ge(qk_low, s.n + 1)
                    if s_next:
                        sp.wait_ge(stack_in[s_next.par], 16 * (MAIN_READS + 1) * (s_next.half + 1))
                    sp.dma_start(parts_dram.rearrange("a p g c -> p a g c"), qk_p[:, :, :, :]).then_inc(parts_out, 16)
                if s_next:
                    s = s_next
                    sp.wait_ge(mt_evac, s.n + 1)
                    for r in range(4):
                        sp.dma_start(stack[s.par][ROW_SELF + r:ROW_SELF + r + 1, :, COL_Q:COL_Q + S],
                                     mT[r * H:(r + 1) * H, :]).then_inc(max_in[s.par], 16)
                if s_tail:
                    s = s_tail
                    sp.wait_ge(o_ready, s.n + 1)
                    sp.dma_start(out[s.n], o_sb[:, :, :]).then_inc(out_done[s.par], 16)

            run(sp, body)
            for p in range(2):
                sp.wait_ge(out_done[p], 16 * (B // 2))

        @block.tensor
        def _(pe):
            pe.wait_ge(w_in, 16 * N_LOADS)
            pe.wait_ge(const_pool, N_CONST_POOL)
            pe.wait_ge(const_dve, N_CONST_DVE)
            pe.wait_ge(const_dma, 16 * N_CONST_DMA)

            def numerators(s, q):
                st = stack[s.par]
                if q == 0:
                    pe.wait_ge(stack_in[s.par], 16 * (MAIN_READS + 1) * (s.half + 1))
                    pe.wait_ge(max_in[s.par], 64 * (s.half + 1))
                for n in range(5):
                    m = 5 * q + n
                    t = tb[m % 2]
                    wait(pe, t_done, T_BANKS * s.n + m - 1)
                    heads = {0: (0, 1), 1: (2, 3), 2: (0, 1, 2, 3), 3: (0, 1), 4: (2, 3)}[n]
                    for a, h4 in enumerate(heads):
                        h = QH * q + h4
                        first, last = a == 0, a == len(heads) - 1
                        if n < 2:
                            mm = nc.tensor.matmul(t[:, a * S:(a + 1) * S], st[0:ROWS, h, COL_K:COL_K + P],
                                                  st[0:ROWS, h, COL_Q:COL_Q + S], start=first, stop=last,
                                                  skip_group_check=True)
                        elif n == 2:
                            mm = nc.tensor.matmul(t[:, a * P:(a + 1) * P], st[0:ROWS, h, COL_K + P:COL_K + S],
                                                  st[0:ROWS, h, COL_Q + P:COL_Q + S], start=first, stop=last,
                                                  skip_group_check=True)
                        else:
                            mm = nc.tensor.matmul(t[0:SE, a * S:(a + 1) * S], st[0:ROWS, h, COL_C:COLS],
                                                  st[0:ROWS, h, COL_Q:COL_Q + S], start=first, stop=last,
                                                  skip_group_check=True)
                    mm.then_inc(t_ready, 1)

            def products(s, q):
                qn = 4 * s.n + q
                pe.wait_ge(pl_self, qn + 1)
                pe.wait_ge(pl_cross, qn + 1)
                if q == 0:
                    pe.wait_ge(v_hi, s.n + 1)
                    pe.wait_ge(v_mid, s.n + 1)
                    pe.wait_ge(v_low, s.n + 1)
                wait(pe, pv_evac, qn)
                if q == QUADS - 1:
                    if not (isinstance(s.n, int) and s.n == B - 1):
                        pe.wait_ge(mt_evac, s.n + 2)
                hi, lo = ph[q % 2], pl[q % 2]
                first = True
                for qb in range(TB):
                    for h4 in range(QH):
                        h = QH * q + h4
                        for a in range(2):
                            u = (qb * QH + h4) * 2 + a
                            out_v1 = ob[:, u * HV:(u + 1) * HV]
                            out_v = ob[:, u * HV:u * HV + HD]
                            if a == 0:
                                blocks = [(0, P, SELF0 + h4 * S + qb * P)]
                                if qb == 1:
                                    blocks.append((1, P, SELF1 + h4 * P))
                            else:
                                blocks = [(2, SE, CROSS + h4 * S + qb * P)]
                            for blk, rows, col in blocks:
                                for w, outs, v in ((hi, out_v1, v1), (hi, out_v, v2), (hi, out_v, v3),
                                                   (lo, out_v1, v1), (lo, out_v, v2)):
                                    mm = nc.tensor.matmul(outs, w[0:rows, col:col + P], v[s.par][0:rows, blk, h, :],
                                                          start=first, stop=False, skip_group_check=True)
                                    first = False
                mm.then_inc(pv_ready, 1)

            def row_scores(s, banks):
                st = stack[s.par]
                R = ROW_SELF
                for m in banks:
                    if m == 0:
                        pe.wait_ge(stack_in[s.par], 16 * (MAIN_READS + 1) * (s.half + 1))
                    t = sbk[m % 2]
                    wait(pe, s_done, S_BANKS * s.n + m - 1)
                    if m < 8:
                        o = t[:, :].rearrange("p (a c) -> p a c", a=2)
                        nc.tensor.matmul(o[:, :, P:S], identb[:, :], causal[:, 0:2, :], start=True, stop=False,
                                         skip_group_check=True)
                        for a in range(2):
                            h = 2 * m + a
                            mm = nc.tensor.matmul(o[:, a, :], st[0:R, h, COL_Q + P:COL_Q + S],
                                                  st[0:R, h, COL_K:COL_K + S], start=False, stop=a == 1,
                                                  skip_group_check=True)
                    elif m < 12:
                        o = t[:, :].rearrange("p (a c) -> p a c", a=4)
                        nc.tensor.matmul(o, identb[:, :], causal[:, :, :], start=True, stop=False,
                                         skip_group_check=True)
                        for a in range(4):
                            h = 4 * (m - 8) + a
                            mm = nc.tensor.matmul(o[:, a, :], st[0:R, h, COL_Q:COL_Q + P],
                                                  st[0:R, h, COL_K:COL_K + P], start=False, stop=a == 3,
                                                  skip_group_check=True)
                    else:
                        qb, run_ = divmod(m - 12, 3)
                        heads = range(CROSS_RUN * run_, min(CROSS_RUN * run_ + CROSS_RUN, H))
                        for a, h in enumerate(heads):
                            mm = nc.tensor.matmul(t[:, a * SE:(a + 1) * SE], st[0:R, h, COL_Q + qb * P:COL_Q + (qb + 1) * P],
                                                  st[0:R, h, COL_C:COLS], start=a == 0, stop=a == len(heads) - 1,
                                                  skip_group_check=True)
                    mm.then_inc(s_ready, 1)

            def max_transposes(s):
                pe.wait_ge(m_low, s.n + 1)
                wait(pe, pv_evac, 4 * s.n - 1)
                for t in range(TB):
                    mm = nc.tensor.matmul(ob[0:4 * H, t * P:(t + 1) * P],
                                          mparts[:, t, :, :, :].rearrange("p a b h -> p (a b h)"), identb[:, :],
                                          start=t == 0, stop=True, skip_group_check=True)
                mm.then_inc(mt_ready, 1)

            def values(s):
                pe.wait_ge(x_in[s.par], 32 * (s.half + 1))
                wait(pe, qk_evac, 6 * (s.n + 1))
                for t in range(TB):
                    for k in range(KC):
                        mm = nc.tensor.matmul(ga[:, t * D:(t + 1) * D], xTs[s.par][:, k, t * P:(t + 1) * P], wv[:, k, :],
                                              start=t == 0 and k == 0, stop=k == KC - 1, skip_group_check=True)
                mm.then_inc(v_ready, 1)
                pe.wait_ge(v_evac, 2 * s.n + 1)
                for k in range(KC):
                    mm = nc.tensor.matmul(ga[0:SE, 0:D], cTs[s.par][:, k, :], wv[:, k, :], start=k == 0, stop=k == KC - 1)
                mm.then_inc(v_ready, 1)

            def queries(s):
                pe.wait_ge(x_in[s.par], 32 * (s.half + 1))
                wait(pe, v_evac, 2 * s.n)
                for which, src, width in ((0, xTs, S), (1, xTs, S), (1, cTs, SE)):
                    step = 0 if which == 0 else 1 if src is xTs else 2
                    if step:
                        pe.wait_ge(qk_evac, 6 * s.n + 2 * step)
                    for g in range(GROUPS):
                        for k in range(KC):
                            mm = nc.tensor.matmul(ga[:, g * width:(g + 1) * width], wqk[:, k, which, g, :],
                                                  src[s.par][:, k, :], start=g == 0 and k == 0, stop=k == KC - 1,
                                                  skip_group_check=True)
                    mm.then_inc(qk_ready, 1)

            def into_gc(s, which, use):
                if which == 0:
                    wait(pe, gc0_evac, 10 * s.n + use)
                else:
                    wait(pe, gc1_evac, 5 * s.n + use)

            def transposes(src, dst):
                for k in range(KC):
                    for t in range(TB):
                        mm = nc.tensor.transpose(dst[:, k * S + t * P:k * S + (t + 1) * P],
                                                 src[:, t, k * P:(k + 1) * P], ident[:, :])
                return mm

            def by_token(dst, lhs, rhs):
                for t in range(TB):
                    for k in range(KC):
                        mm = nc.tensor.matmul(dst[:, t * D:(t + 1) * D], lhs[:, k, t * P:(t + 1) * P], rhs[:, k, :],
                                              start=t == 0 and k == 0, stop=k == KC - 1, skip_group_check=True)
                return mm

            def mlp(s_tail, s_next):
                n = s_tail.n if s_tail else None

                def up(j):
                    into_gc(s_tail, 0, 2 + j)
                    if j == 0:
                        pe.wait_ge(gc0_evac, 10 * n + 2)
                    for c in range(2):
                        for k in range(KC):
                            f = 2 * j + c
                            mm = nc.tensor.matmul(gc[0][:, c * S:(c + 1) * S], wfc[:, k, f * P:(f + 1) * P], nT[:, k, :],
                                                  start=c == 0 and k == 0, stop=k == KC - 1, skip_group_check=True)
                    mm.then_inc(gc0_ready, 1)

                def down(j):
                    pe.wait_ge(gelu_done, 8 * n + 2 * j + 2)
                    for f in (2 * j, 2 * j + 1):
                        for t in range(TB):
                            mm = nc.tensor.matmul(gc[1][:, t * D:(t + 1) * D], hid[:, f, t * P:(t + 1) * P], wm[:, f, :],
                                                  start=f == 0 and t == 0, stop=f == FC - 1, skip_group_check=True)
                    if j == 3:
                        mm.then_inc(gc1_ready, 1)

                if s_tail:
                    up(0)
                if s_next:
                    row_scores(s_next, range(0, 2))
                if s_tail:
                    up(1)
                    into_gc(s_tail, 1, 1)
                    down(0)
                if s_next:
                    row_scores(s_next, range(2, 5))
                if s_tail:
                    up(2)
                    down(1)
                if s_next:
                    row_scores(s_next, range(5, 8))
                if s_tail:
                    up(3)
                    down(2)
                if s_next:
                    row_scores(s_next, range(8, 12))
                if s_tail:
                    down(3)

            def body(i, at):
                c, a, b, q = seqs(i, at)
                if a:
                    numerators(a, 0)
                if b:
                    values(b)
                if c:
                    pe.wait_ge(att_ready, 4 * c.n + 4)
                    into_gc(c, 0, 0)
                    transposes(att[:, :, :, :].rearrange("p t h d -> p t (h d)"), gc[0]).then_inc(gc0_ready, 1)
                if a:
                    numerators(a, 1)
                if c:
                    pe.wait_ge(gc0_evac, 10 * c.n + 1)
                    into_gc(c, 1, 0)
                    by_token(gc[1], attT, wo).then_inc(gc1_ready, 1)
                if q:
                    queries(q)
                if a:
                    products(a, 0)
                if c:
                    pe.wait_ge(n_ready, 2 * c.n + 2)
                    into_gc(c, 0, 1)
                    transposes(n1, gc[0]).then_inc(gc0_ready, 1)
                mlp(c, b)
                if a:
                    products(a, 1)
                    numerators(a, 2)
                if c:
                    pe.wait_ge(h_ready, 2 * c.n + 2)
                    into_gc(c, 0, 6)
                    transposes(h1, gc[0]).then_inc(gc0_ready, 1)
                if b:
                    row_scores(b, range(12, 15))
                if c:
                    pe.wait_ge(gc0_evac, 10 * c.n + 7)
                    pe.wait_ge(tok_in[c.par], 48 * (c.half + 1))
                    for t in range(TB):
                        for k in range(KC):
                            mm = nc.tensor.matmul(gc[0][:, t * SE:(t + 1) * SE], hT[:, k, t * P:(t + 1) * P],
                                                  cTt[c.par][:, k, :], start=t == 0 and k == 0, stop=k == KC - 1,
                                                  skip_group_check=True)
                    mm.then_inc(gc0_ready, 1)
                if a:
                    numerators(a, 3)
                    products(a, 2)
                if c:
                    pe.wait_ge(p2_ready, 2 * c.n + 2)
                    into_gc(c, 1, 2)
                    for t in range(TB):
                        mm = nc.tensor.transpose(gc[1][0:SE, t * P:(t + 1) * P], p2[:, t, :], ident[:, :])
                    mm.then_inc(gc1_ready, 1)
                if b:
                    row_scores(b, range(15, 18))
                if c:
                    pe.wait_ge(gc1_evac, 5 * c.n + 3)
                    into_gc(c, 0, 8)
                    for t in range(TB):
                        mm = nc.tensor.matmul(gc[0][:, t * D:(t + 1) * D], p2T[:, t * P:(t + 1) * P], ct[c.par][:, :],
                                              start=t == 0, stop=True, skip_group_check=True)
                    mm.then_inc(gc0_ready, 1)
                if b:
                    max_transposes(b)
                if c:
                    pe.wait_ge(x2_ready, 2 * c.n + 2)
                    into_gc(c, 1, 3)
                    transposes(x2, gc[1]).then_inc(gc1_ready, 1)
                    pe.wait_ge(gc1_evac, 5 * c.n + 4)
                    into_gc(c, 0, 9)
                    for f in range(KC):
                        for k in range(KC):
                            mm = nc.tensor.matmul(gc[0][:, f * S:(f + 1) * S], w1s[:, k, f * P:(f + 1) * P], x2T[:, k, :],
                                                  start=f == 0 and k == 0, stop=k == KC - 1, skip_group_check=True)
                    mm.then_inc(gc0_ready, 1)
                if a:
                    products(a, 3)
                if c:
                    pe.wait_ge(gc0_evac, 10 * c.n + 10)
                    into_gc(c, 1, 4)
                    by_token(gc[1], r2T, w2s).then_inc(gc1_ready, 1)

            run(pe, body)

        @block.scalar
        def _(act):
            act.wait_ge(w_in, 16 * N_LOADS)

            def exps(s, q):
                qn = 4 * s.n + q
                wait(act, pl_self, qn - 1)
                wait(act, pl_cross, qn - 1)
                dst = pf[q % 2]
                for n, (rows, col) in enumerate(((P, SELF0), (P, SELF0 + 512), (P, SELF1), (SE, CROSS), (SE, CROSS + 512))):
                    m = 5 * q + n
                    act.wait_ge(t_ready, T_BANKS * s.n + m + 1)
                    nc.scalar.activation(dst[0:rows, col:col + 512], tb[m % 2][0:rows, :], ACT.Exp,
                                         scale=HD ** -0.5).then_inc(t_done, 1)

            def highs(s, q):
                qn = 4 * s.n + q
                wait(act, pv_ready, qn - 1)
                act.wait_ge(causal_done, 2 * qn + 2)
                nc.scalar.activation(ph[q % 2][:, 0:CROSS], pf[q % 2][:, 0:CROSS], ACT.Copy).then_inc(p_hi, 1)
                act.wait_ge(t_done, T_BANKS * s.n + 5 * q + 5)
                nc.scalar.activation(ph[q % 2][0:SE, CROSS:QUAD_COLS], pf[q % 2][0:SE, CROSS:QUAD_COLS],
                                     ACT.Copy).then_inc(p_hi, 1)

            def from_gc(s, which, use, dst, src):
                if which == 0:
                    act.wait_ge(gc0_ready, 10 * s.n + use)
                    nc.scalar.activation(dst, src, ACT.Copy).then_inc(gc0_evac, 1)
                else:
                    act.wait_ge(gc1_ready, 5 * s.n + use)
                    nc.scalar.activation(dst, src, ACT.Copy).then_inc(gc1_evac, 1)

            def flat(t):
                return t[:, :, :].rearrange("p k s -> p (k s)")

            def body(i, at):
                c, a, b, q = seqs(i, at)
                if a:
                    exps(a, 0)
                if c:
                    from_gc(c, 0, 1, flat(attT), gc[0][:, :])
                if a:
                    highs(a, 0)
                    exps(a, 1)
                    highs(a, 1)
                if q:
                    wait(act, qk_hi, q.n)
                    wait(act, qk_rest, q.n)
                    for step, (which, col, width) in enumerate(((0, COL_Q, S), (1, COL_K, S), (1, COL_C, SE))):
                        act.wait_ge(qk_ready, 3 * q.n + step + 1)
                        for g in range(GROUPS):
                            nc.scalar.activation(qk_f[:, g, col:col + width], ga[:, g * width:(g + 1) * width], ACT.Identity,
                                                 bias=bqk[:, which, g:g + 1]).then_inc(qk_evac, 1)
                if c:
                    from_gc(c, 0, 2, flat(nT), gc[0][:, :])
                    for j in range(4):
                        act.wait_ge(gc0_ready, 10 * c.n + 3 + j)
                        if j == 0:
                            wait(act, gc1_ready, 5 * (c.n - 1) + 2)
                        for e in range(2):
                            f = 2 * j + e
                            ins = nc.scalar.activation(hid[:, f, :], gc[0][:, e * S:(e + 1) * S], ACT.Gelu_apprx_tanh,
                                                       bias=bfc[:, f:f + 1])
                            ins.then_inc(gelu_done, 1)
                        act.wait_ge(gelu_done, 8 * c.n + 2 * j + 2)
                        nc.scalar.activation(tick[:, 0:1], bfc[:, 0:1], ACT.Copy).then_inc(gc0_evac, 1)
                if a:
                    exps(a, 2)
                if c:
                    from_gc(c, 0, 7, flat(hT), gc[0][:, :])
                if a:
                    highs(a, 2)
                if c:
                    act.wait_ge(nm_ready, c.n + 1)
                    wait(act, gc1_ready, 5 * (c.n - 1) + 3)
                    wait(act, rden2_ready, c.n)
                    for t in range(TB):
                        nc.scalar.activation(p2[:, t, :], gc[0][:, t * SE:(t + 1) * SE], ACT.Exp, scale=D ** -0.5,
                                             bias=nms[:, t:t + 1], accum_out=den2[:, t:t + 1]).then_inc(p2_ready, 1)
                    act.wait_ge(p2_ready, 2 * c.n + 2)
                    nc.scalar.activation(tick[:, 1:2], bfc[:, 0:1], ACT.Copy).then_inc(gc0_evac, 1)
                if a:
                    exps(a, 3)
                    highs(a, 3)
                if c:
                    from_gc(c, 1, 3, p2T[:, :], gc[1][0:SE, 0:S])
                if b:
                    act.wait_ge(mt_ready, b.n + 1)
                    wait(act, max_in[1 - b.par], 64 * (b.half + b.par))
                    nc.scalar.activation(mT[:, :], ob[0:4 * H, 0:S], ACT.Copy).then_inc(mt_evac, 1)
                if c:
                    from_gc(c, 1, 4, flat(x2T), gc[1][:, :])
                    act.wait_ge(gc0_ready, 10 * c.n + 10)
                    nc.scalar.activation(r2T[:, 0, :], gc[0][:, 0:S], ACT.Relu, bias=b1s[:, 0:1]).then_inc(relu_half, 1)
                    nc.scalar.activation(r2T[:, 1, :], gc[0][:, S:2 * S], ACT.Relu, bias=b1s[:, 1:2]).then_inc(relu_half, 1)
                    act.wait_ge(relu_half, 2 * c.n + 2)
                    nc.scalar.activation(tick[:, 2:3], bfc[:, 0:1], ACT.Copy).then_inc(gc0_evac, 1)

            run(act, body)

        @block.vector
        def _(dve):
            v = nc.vector
            v.memset(rows01[:, 0, :], 0.0).then_inc(const_dve, 1)
            v.memset(rows01[:, 1, :], 1.0).then_inc(const_dve, 1)
            dve.wait_ge(mask_in, 16)
            v.tensor_copy(mask_f[:, :], mask_i[:, :]).then_inc(mask_float, 1)
            dve.wait_ge(mask_float, 1)
            v.tensor_scalar(mask_p[:, 0, :], mask_f[:, :], -99840.0 * HD ** 0.5, None, ALU.mult)
            v.tensor_scalar(mask_p[:, 1, :], mask_f[:, :], (NEG + 99840.0) * HD ** 0.5, None, ALU.mult).then_inc(const_dve, 1)
            v.memset(half_pow[:, :], -0.5).then_inc(const_dve, 1)
            for p in range(2):
                v.memset(v1[p][:, :, :, HD:HV], 1.0).then_inc(const_dve, 1)
            v.memset(v_f[:, 2, :], 0.0).then_inc(const_dve, 1)
            dve.wait_ge(w_in, 16 * N_LOADS)
            v.tensor_scalar(wo[:, :, :], wo[:, :, :], 0.5, None, ALU.mult).then_inc(const_dve, 1)
            dve.wait_ge(const_dve, N_CONST_DVE)
            dve.wait_ge(const_pool, N_CONST_POOL)

            def heads(t, blk=slice(0, 3)):
                return t[:, blk, :].rearrange("p b (h d) -> p (b h) d", d=HD)

            def low_self(s, q):
                qn = 4 * s.n + q
                dve.wait_ge(p_hi, 2 * qn + 1)
                v.tensor_tensor(pl[q % 2][:, 0:CROSS], pf[q % 2][:, 0:CROSS], ph[q % 2][:, 0:CROSS],
                                ALU.subtract).then_inc(pl_self, 1)

            def norm(s, q):
                qn = 4 * s.n + q
                o = ob[:, 0:UNITS * HV].rearrange("p (u c) -> p u c", c=HV)
                dve.wait_ge(pv_ready, qn + 1)
                v.reciprocal(rden[:, :], o[:, :, HD]).then_inc(rden_ready, 1)
                dve.wait_ge(rden_ready, qn + 1)
                wait(dve, att_ready, qn)
                r = rden[:, :]
                rb = bass.AP(r.tensor, r.offset, [[UNITS, P], [1, UNITS], [0, HD]])
                v.tensor_tensor(onorm[:, :, :], o[:, :, 0:HD], rb, ALU.mult).then_inc(pv_evac, 1)
                dve.wait_ge(pv_evac, qn + 1)
                if q == 0:
                    wait(dve, gc0_ready, 10 * (s.n - 1) + 1)
                on = onorm[:, :, :].rearrange("p (t h a) d -> p a t h d", t=TB, a=2)
                for t in range(TB):
                    ins = v.tensor_tensor(att[:, t, QH * q:QH * q + QH, :], on[:, 0, t], on[:, 1, t], ALU.add)
                ins.then_inc(att_ready, 1)

            def row_max(s, banks):
                for m in banks:
                    dve.wait_ge(s_ready, S_BANKS * s.n + m + 1)
                    if m == 0:
                        wait(dve, m_low, s.n)
                    t = sbk[m % 2]
                    if m < 8:
                        src, dst = t[:, :].rearrange("p (a c) -> p a c", a=2), mx[:, 1, 0, 2 * m:2 * m + 2]
                    elif m < 12:
                        src, dst = t[:, :].rearrange("p (a c) -> p a c", a=4), mx[:, 0, 0, 4 * (m - 8):4 * (m - 7)]
                    else:
                        qb, run_ = divmod(m - 12, 3)
                        h0, h1_ = CROSS_RUN * run_, min(CROSS_RUN * run_ + CROSS_RUN, H)
                        src = t[:, 0:(h1_ - h0) * SE].rearrange("p (a c) -> p a c", c=SE)
                        dst = mx[:, qb, 1, h0:h1_]
                    v.tensor_reduce(dst, src, AX_X, ALU.max, negate=True).then_inc(s_done, 1)

            def max_parts(s):
                dve.wait_ge(s_done, S_BANKS * (s.n + 1))
                wait(dve, mt_ready, s.n)
                for t in range(TB):
                    ins = v.tensor_copy(mparts[:, t, :, 0, :], mx[:, t, :, :])
                ins.then_inc(m_hi, 1)
                dve.wait_ge(m_hi, s.n + 1)
                for t in range(TB):
                    ins = v.tensor_tensor(mparts[:, t, :, 1, :], mx[:, t, :, :], mparts[:, t, :, 0, :], ALU.subtract)
                ins.then_inc(m_low, 1)

            def layer_stats(s, src, ln):
                for t in range(TB):
                    v.bn_stats(stats[:, t, :], src[:, t, :]).then_inc(stat_ready, 1)
                dve.wait_ge(stat_ready, 4 * s.n + 2 * ln + 2)
                v.memset(tick[:, 3:4], 0.0)
                for t in range(TB):
                    v.bn_aggr(mv[:, t, :], stats[:, t, :]).then_inc(mv_ready, 1)
                dve.wait_ge(mv_ready, 4 * s.n + 2 * ln + 2)
                v.tensor_scalar(ve[:, :], mv[:, :, 1], EPS, None, ALU.add).then_inc(ve_ready, 1)

            def layer_scale(s, src, gamma, ln):
                for t in range(TB):
                    v.scalar_tensor_tensor(scaled[:, t, :], src[:, t, :], mv[:, t, 0:1], gamma[:, :],
                                           ALU.subtract, ALU.mult).then_inc(scaled_ready, 1)

            def layer_out(s, dst, beta, ln, done):
                dve.wait_ge(scaled_ready, 4 * s.n + 2 * ln + 2)
                dve.wait_ge(rstd_ready, 2 * s.n + ln + 1)
                for t in range(TB):
                    v.scalar_tensor_tensor(dst[:, t, :], scaled[:, t, :], rstd[:, t:t + 1], beta[:, :],
                                           ALU.mult, ALU.add).then_inc(done, 1)

            def both(t):
                return t[:, :, :].rearrange("p t d -> p (t d)")

            def body(i, at):
                c, a, b, q = seqs(i, at)
                if b:
                    dve.wait_ge(v_ready, 2 * b.n + 1)
                    wait(dve, v_rest, b.n)
                    wait(dve, v_hi, b.n)
                    v.tensor_tensor(both(v_f[:, 0:2, :]), ga[:, :], both(bv2), ALU.add).then_inc(v_evac, 1)
                    dve.wait_ge(v_ready, 2 * b.n + 2)
                    v.tensor_tensor(v_f[0:SE, 2, :], ga[0:SE, 0:D], bv2[0:SE, 0, :], ALU.add).then_inc(v_evac, 1)
                    dve.wait_ge(v_evac, 2 * b.n + 2)
                    wait(dve, pv_ready, 4 * (b.n - 1))
                    v.tensor_copy(v1[b.par][:, :, :, 0:HD].rearrange("p b h d -> p (b h) d"), heads(v_f)).then_inc(v_hi, 1)
                if a:
                    low_self(a, 0)
                if c:
                    dve.wait_ge(gc1_ready, 5 * c.n + 1)
                    dve.wait_ge(xb_ready, c.n + 1)
                    v.tensor_tensor(both(y), gc[1][:, :], both(xb), ALU.add).then_inc(gc1_evac, 1)
                    dve.wait_ge(gc1_evac, 5 * c.n + 1)
                    layer_stats(c, y, 0)
                    dve.wait_ge(mv_ready, 4 * c.n + 2)
                    layer_scale(c, y, g1s, 0)
                if b:
                    dve.wait_ge(v_rest, b.n + 1)
                    v.tensor_copy(v2[b.par][:, :, :, :].rearrange("p b h d -> p (b h) d"), heads(v_r)).then_inc(v_mid, 1)
                if a:
                    low_self(a, 1)
                if c:
                    layer_out(c, n1, be1s, 0, n_ready)
                if a:
                    norm(a, 0)
                if q:
                    dve.wait_ge(qk_evac, 6 * (q.n + 1))
                    wait(dve, parts_out, 16 * q.n)
                    v.tensor_copy(qk_p[:, 0, :, :], qk_f[:, :, :]).then_inc(qk_hi, 1)
                if b:
                    row_max(b, range(0, 6))
                if q:
                    dve.wait_ge(qk_rest, q.n + 1)
                    v.tensor_copy(qk_p[:, 1, :, :], qk_r[:, :, :]).then_inc(qk_mid, 1)
                if b:
                    row_max(b, range(6, 12))
                if c:
                    dve.wait_ge(gc1_ready, 5 * c.n + 2)
                    dve.wait_ge(nb_ready, c.n + 1)
                    v.tensor_tensor(both(z), gc[1][:, :], both(nb), ALU.add).then_inc(gc1_evac, 1)
                    dve.wait_ge(gc1_evac, 5 * c.n + 2)
                    layer_stats(c, z, 1)
                    dve.wait_ge(mv_ready, 4 * c.n + 4)
                    layer_scale(c, z, g2s, 1)
                if a:
                    norm(a, 1)
                if c:
                    layer_out(c, h1, be2s, 1, h_ready)
                if b:
                    row_max(b, range(12, 15))
                if a:
                    low_self(a, 2)
                if c:
                    dve.wait_ge(gc0_ready, 10 * c.n + 8)
                    v.tensor_reduce(nm[:, :], gc[0][:, 0:TB * SE].rearrange("p (t c) -> p t c", t=TB), AX_X, ALU.max,
                                    negate=True).then_inc(nm_raw, 1)
                    dve.wait_ge(nm_raw, c.n + 1)
                    v.tensor_scalar(nms[:, :], nm[:, :], D ** -0.5, None, ALU.mult).then_inc(nm_ready, 1)
                if a:
                    low_self(a, 3)
                    norm(a, 2)
                if b:
                    row_max(b, range(15, 18))
                    max_parts(b)
                if c:
                    dve.wait_ge(p2_ready, 2 * c.n + 2)
                    v.reciprocal(rden2[:, :], den2[:, :]).then_inc(rden2_ready, 1)
                    dve.wait_ge(rden2_ready, c.n + 1)
                    dve.wait_ge(gc0_ready, 10 * c.n + 9)
                    for t in range(TB):
                        v.scalar_tensor_tensor(x2[:, t, :], gc[0][:, t * D:(t + 1) * D], rden2[:, t:t + 1], h1[:, t, :],
                                               ALU.mult, ALU.add).then_inc(x2_ready, 1)
                    dve.wait_ge(x2_ready, 2 * c.n + 2)
                    v.memset(tick[:, 3:4], 0.0).then_inc(gc0_evac, 1)
                if a:
                    norm(a, 3)
                if c:
                    dve.wait_ge(gc1_ready, 5 * c.n + 5)
                    dve.wait_ge(x2b_ready, c.n + 1)
                    wait(dve, out_done[1 - c.par], 16 * (c.half + c.par))
                    v.tensor_tensor(both(o_sb), gc[1][:, :], both(x2b), ALU.add).then_inc(gc1_evac, 1)
                    dve.wait_ge(gc1_evac, 5 * c.n + 5)
                    v.memset(tick[:, 3:4], 0.0).then_inc(o_ready, 1)

            run(dve, body)

        @block.gpsimd
        def _(pool):
            g = nc.gpsimd
            g.memset(ident[:, :], 0.0).then_inc(const_pool, 1)
            g.memset(identb[:, :], 0.0).then_inc(const_pool, 1)
            g.memset(causal[:, :, :], -1e30).then_inc(const_pool, 1)
            g.memset(ptick[:, :], 0.0).then_inc(const_pool, 1)
            pool.wait_ge(const_pool, 4)
            for m in (ident, identb):
                g.affine_select(out=m[:, :], in_=m[:, :], compare_op=ALU.not_equal, fill=1.0, base=0,
                                pattern=[[-1, P]], channel_multiplier=1).then_inc(const_pool, 1)
            g.affine_select(out=causal[:, :, :], in_=causal[:, :, :], compare_op=ALU.is_gt, fill=0.0, base=0,
                            pattern=[[0, 4], [1, P]], channel_multiplier=-1).then_inc(const_pool, 1)
            pool.wait_ge(const_dve, N_CONST_DVE)
            pool.wait_ge(w_in, 16 * N_LOADS)
            pool.wait_ge(const_pool, N_CONST_POOL)

            def carry():
                g.tensor_tensor(ptick[:, 0:1], ptick[:, 1:2], ptick[:, 2:3], ALU.add)

            def clear_masked(s, q):
                pool.wait_ge(t_done, T_BANKS * s.n + 5 * q + 3)
                carry()
                d0 = pf[q % 2][:, SELF0:SELF1].rearrange("p (h c) -> p h c", h=QH)[:, :, 0:P]
                d1 = pf[q % 2][:, SELF1:CROSS].rearrange("p (h c) -> p h c", h=QH)
                for d in (d0, d1):
                    g.affine_select(out=d, in_=d, compare_op=ALU.is_ge, fill=0.0, base=0,
                                    pattern=[[0, QH], [1, P]], channel_multiplier=-1).then_inc(causal_done, 1)

            def low_cross(s, q):
                qn = 4 * s.n + q
                pool.wait_ge(p_hi, 2 * qn + 2)
                g.tensor_tensor(pl[q % 2][0:SE, CROSS:QUAD_COLS], pf[q % 2][0:SE, CROSS:QUAD_COLS],
                                ph[q % 2][0:SE, CROSS:QUAD_COLS], ALU.subtract).then_inc(pl_cross, 1)

            def heads(t):
                return t.rearrange("p b (h d) -> p (b h) d", d=HD)

            def body(i, at):
                c, a, b, q = seqs(i, at)
                if c:
                    pool.wait_ge(tok_in[c.par], 48 * (c.half + 1))
                    wait(pool, gc1_evac, 5 * (c.n - 1) + 1)
                    g.tensor_tensor(xb[:, :, :], xt[c.par][:, :, :], bo2[:, :, :], ALU.add).then_inc(xb_ready, 1)
                if a:
                    clear_masked(a, 0)
                if b:
                    pool.wait_ge(v_hi, b.n + 1)
                    wait(pool, v_mid, b.n)
                    g.tensor_tensor(heads(v_r[:, :, :]), heads(v_f[:, :, :]),
                                    v1[b.par][:, :, :, 0:HD].rearrange("p b h d -> p (b h) d"),
                                    ALU.subtract).then_inc(v_rest, 1)
                if a:
                    low_cross(a, 0)
                    clear_masked(a, 1)
                if c:
                    pool.wait_ge(ve_ready, 2 * c.n + 1)
                    g.tensor_tensor(rstd[:, :], ve[:, :], half_pow[:, :], ALU.pow).then_inc(rstd_ready, 1)
                if b:
                    pool.wait_ge(v_mid, b.n + 1)
                    g.tensor_tensor(v3[b.par][:, :, :, :].rearrange("p b h d -> p (b h) d"), heads(v_r[:, :, :]),
                                    v2[b.par][:, :, :, :].rearrange("p b h d -> p (b h) d"),
                                    ALU.subtract).then_inc(v_low, 1)
                if a:
                    low_cross(a, 1)
                if q:
                    pool.wait_ge(qk_hi, q.n + 1)
                    g.tensor_tensor(qk_r[:, :, :], qk_f[:, :, :], qk_p[:, 0, :, :], ALU.subtract).then_inc(qk_rest, 1)
                if c:
                    pool.wait_ge(n_ready, 2 * c.n + 2)
                    wait(pool, gc1_evac, 5 * (c.n - 1) + 2)
                    g.tensor_tensor(nb[:, :, :], n1[:, :, :], bm2[:, :, :], ALU.add).then_inc(nb_ready, 1)
                if q:
                    pool.wait_ge(qk_mid, q.n + 1)
                    g.tensor_tensor(qk_p[:, 2, :, :], qk_r[:, :, :], qk_p[:, 1, :, :], ALU.subtract).then_inc(qk_low, 1)
                if c:
                    pool.wait_ge(ve_ready, 2 * c.n + 2)
                    g.tensor_tensor(rstd[:, :], ve[:, :], half_pow[:, :], ALU.pow).then_inc(rstd_ready, 1)
                if a:
                    clear_masked(a, 2)
                    low_cross(a, 2)
                    clear_masked(a, 3)
                    low_cross(a, 3)
                if c:
                    pool.wait_ge(x2_ready, 2 * c.n + 2)
                    wait(pool, gc1_evac, 5 * c.n)
                    g.tensor_tensor(x2b[:, :, :], x2[:, :, :], b22[:, :, :], ALU.add).then_inc(x2b_ready, 1)

            run(pool, body)


N_LOADS = 22
N_CONST_DMA = 2 * (2 * 2 + 4 * 2) + 1
N_CONST_POOL = 7
N_CONST_DVE = 8


def kernel(x, ctx_1024, mask_BxS2_ik0, L0_xattn_w_attn, L0_xattn_b_attn, L0_xattn_w_oproj, L0_xattn_b_oproj,
           L0_xattn_w_fc, L0_xattn_b_fc, L0_xattn_w_mproj, L0_xattn_b_mproj, L0_xattn_ln1_g, L0_xattn_ln1_b,
           L0_xattn_ln2_g, L0_xattn_ln2_b, L1_xattn_W1, L1_xattn_b1, L1_xattn_W2, L1_xattn_b2):
    import concourse.bacc as bacc
    from concourse.bass_utils import run_bass_kernel_spmd

    def chunks(w):
        w = np.asarray(w)
        return w.reshape(-1, P, w.shape[1]).transpose(1, 0, 2)

    def columns(b):
        return np.asarray(b).reshape(-1, P).T

    def head_groups(w):
        w = np.asarray(w)
        return w.reshape(*w.shape[:-1], GH, GROUPS, HD).swapaxes(-3, -2).swapaxes(-1, -2).reshape(
            *w.shape[:-1], GROUPS, P)

    xs, cs, wa, ba = (np.asarray(t) for t in (x, ctx_1024, L0_xattn_w_attn, L0_xattn_b_attn))
    w_qk = np.stack([head_groups(wa[:, :D]), head_groups(wa[:, D:2 * D])], 1)
    b_qk = np.stack([head_groups(ba[:D]), head_groups(ba[D:2 * D])], 0)
    arrays = {
        "x_tok": xs.reshape(B, TB, P, D).transpose(0, 2, 1, 3),
        "x_chan": xs.transpose(0, 2, 1).reshape(B, KC, P, S).transpose(0, 2, 1, 3),
        "ctx_tok": cs,
        "ctx_chan": cs.transpose(0, 2, 1).reshape(B, KC, P, SE).transpose(0, 2, 1, 3),
        "mask": np.asarray(mask_BxS2_ik0),
        "w_qk": w_qk.reshape(KC, P, 2, GROUPS, P).transpose(1, 0, 2, 3, 4),
        "b_qk": b_qk.transpose(2, 0, 1),
        "w_v": chunks(wa[:, 2 * D:]),
        "b_v": ba[2 * D:],
        "w_o": chunks(L0_xattn_w_oproj),
        "b_o": L0_xattn_b_oproj,
        "w_fc": chunks(L0_xattn_w_fc),
        "b_fc": columns(L0_xattn_b_fc),
        "w_m": chunks(L0_xattn_w_mproj),
        "b_m": L0_xattn_b_mproj,
        "g1": L0_xattn_ln1_g,
        "be1": L0_xattn_ln1_b,
        "g2": L0_xattn_ln2_g,
        "be2": L0_xattn_ln2_b,
        "w1T": chunks(np.asarray(L1_xattn_W1).T),
        "b1": columns(L1_xattn_b1),
        "w2T": chunks(np.asarray(L1_xattn_W2).T),
        "b2": L1_xattn_b2,
    }
    arrays = {f"in_{k}": np.ascontiguousarray(np.asarray(v)) for k, v in arrays.items()}
    nc = bacc.Bacc("TRN2", target_bir_lowering=False, num_devices=1)
    args = [nc.dram_tensor(k, v.shape, mybir.dt.from_np(v.dtype), kind="ExternalInput").ap() for k, v in arrays.items()]
    args.append(nc.dram_tensor("out_0", (B, P, TB, D), F32, kind="ExternalOutput").ap())
    build(nc, *args)
    got = run_bass_kernel_spmd(nc, [arrays], core_ids=[0]).results[0]["out_0"]
    return np.ascontiguousarray(got.transpose(0, 2, 1, 3).reshape(B, S, D))
```

```python
from contextlib import ExitStack

import numpy as np

import concourse.bass as bass
from concourse import mybir

ALU = mybir.AluOpType
ACT = mybir.ActivationFunctionType
F32 = mybir.dt.float32
BF16 = mybir.dt.bfloat16
F16 = mybir.dt.float16
I32 = mybir.dt.int32
AX_X = mybir.AxisListType.X

P = 128
B, S, D = 32, 256, 256
SE = 77
H, HD = 16, 16
F = 4 * D
KC = D // P
TB = S // P
FC = F // P
QH = 4
QUADS = H // QH
EPS = 1e-5
NEG = -100000.0

Q_PARTS = (0, 1, 2, 0, 1, 0)
K_PARTS = (0, 0, 0, 1, 1, 2)
SLOTS = len(Q_PARTS)
ROW_MASK = SLOTS * HD
ROW_SELF = ROW_MASK + 2
ROW_CROSS = ROW_SELF + 2
ROWS = ROW_CROSS + 2
COL_Q, COL_K, COL_C = 0, S, 2 * S
COLS = 2 * S + SE
GROUPS = 2
GH = H // GROUPS

SELF0, SELF1, CROSS = 0, QH * S, QH * S + QH * P
QUAD_COLS = CROSS + QH * S
V_PARTS = 3
HV = V_PARTS * HD + 1
HALF_UNITS = QH * 2
UNITS = TB * HALF_UNITS
CROSS_RUN = 6
S_BANKS = 8 + 4 + 2 * 3
T_BANKS = 5 * QUADS
SC_BANKS = 4
MAIN_READS = 9


class Seq:

    def __init__(self, n, half, par):
        self.n, self.half, self.par = n, half, par


def wait(eng, sem, value):
    if not (isinstance(value, int) and value <= 0):
        eng.wait_ge(sem, value)


def build(nc, x, xT, ctx_t, ctxT, mask, w_qk, b_qk, w_v, b_v, w_o, b_o, w_fc, b_fc, w_m, b_m,
          g1, be1, g2, be2, w1T, b1, w2T, b2, out):
    ctx = ExitStack()
    with ctx:
        def sb(name, shape, dt=F32):
            return ctx.enter_context(nc.sbuf_tensor(name, shape, dt))

        def bank(name):
            return ctx.enter_context(nc.psum_tensor(name, [P, 512], F32))

        def sem(name):
            return ctx.enter_context(nc.semaphore(name))

        parts_dram = nc.dram_tensor("parts_scratch", (3, P, GROUPS, COLS), BF16, kind="Internal").ap()
        mask_dram = nc.dram_tensor("mask_scratch", (B, 2, SE), BF16, kind="Internal").ap()

        wqk = sb("wqk", [P, KC, 2, GROUPS, P])
        bqk = sb("bqk", [P, 2, GROUPS])
        wv = sb("wv", [P, KC, D])
        wo = sb("wo", [P, KC, D])
        wfc = sb("wfc", [P, KC, F])
        bfc = sb("bfc", [P, FC])
        wm = sb("wm", [P, FC, D])
        w1s = sb("w1s", [P, KC, D])
        b1s = sb("b1s", [P, KC])
        w2s = sb("w2s", [P, KC, D])
        bv2, bo2, bm2, b22 = (sb(n, [P, TB, D]) for n in ("bv2", "bo2", "bm2", "b22"))
        g1s, be1s, g2s, be2s = (sb(n, [P, D]) for n in ("g1s", "be1s", "g2s", "be2s"))
        ident = sb("ident", [P, P])
        identb = sb("identb", [P, P], BF16)
        causal = sb("causal", [P, 4, P], BF16)
        half_pow = sb("half_pow", [P, TB])
        rows01 = sb("rows01", [1, 2, S], BF16)
        mask_i = sb("mask_i", [B, SE], I32)
        mask_f = sb("mask_f", [B, SE])
        mask_p = sb("mask_p", [B, 2, SE], BF16)
        ptick = sb("ptick", [P, 2 + QUADS])
        tick = sb("tick", [P, 4])

        xTs = [sb(f"xTs{p}", [P, KC, S]) for p in range(2)]
        cTs = [sb(f"cTs{p}", [P, KC, SE]) for p in range(2)]
        xt = [sb(f"xt{p}", [P, TB, D]) for p in range(2)]
        ct = [sb(f"ct{p}", [SE, D]) for p in range(2)]
        cTt = [sb(f"cTt{p}", [P, KC, SE]) for p in range(2)]
        stack = [sb(f"stack{p}", [ROWS, H, COLS], BF16) for p in range(2)]
        qk_f = sb("qk_f", [P, GROUPS, COLS])
        qk_r = sb("qk_r", [P, GROUPS, COLS])
        qk_p = sb("qk_p", [P, 3, GROUPS, COLS], BF16)
        v_f = sb("v_f", [P, 3, D])
        v_r = sb("v_r", [P, 3, D])
        vp = sb("vp", [P, 3, H, HV], BF16)
        mx = sb("mx", [P, TB, 2, H])
        mparts = sb("mparts", [P, TB, 2, 2, H], BF16)
        mT = sb("mT", [4 * H, S], BF16)
        pf = [sb(f"pf{p}", [P, QUAD_COLS]) for p in range(2)]
        ph = [sb(f"ph{p}", [P, QUAD_COLS], F16) for p in range(2)]
        pl = [sb(f"pl{p}", [P, QUAD_COLS], F16) for p in range(2)]
        osum = sb("osum", [P, UNITS, HD])
        rden = sb("rden", [P, UNITS])
        onorm = sb("onorm", [P, UNITS, HD])
        att = sb("att", [P, TB, H, HD])
        attT = sb("attT", [P, KC, S])
        xb = sb("xb", [P, TB, D])
        y = sb("y", [P, TB, D])
        stats = sb("stats", [P, TB, 6])
        mv = sb("mv", [P, TB, 2])
        ve = sb("ve", [P, TB])
        rstd = sb("rstd", [P, TB])
        scaled = sb("scaled", [P, TB, D])
        n1 = sb("n1", [P, TB, D])
        nT = sb("nT", [P, KC, S])
        nb = sb("nb", [P, TB, D])
        hid = sb("hid", [P, FC, S])
        z = y
        h1 = sb("h1", [P, TB, D])
        hT = sb("hT", [P, KC, S])
        nm = sb("nm", [P, TB])
        nms = sb("nms", [P, TB])
        p2 = sb("p2", [P, TB, SE])
        den2 = sb("den2", [P, TB])
        rden2 = sb("rden2", [P, TB])
        p2T = sb("p2T", [SE, S])
        x2 = sb("x2", [P, TB, D])
        x2T = sb("x2T", [P, KC, S])
        x2b = n1
        r2T = sb("r2T", [P, KC, S])
        o_sb = sb("o_sb", [P, TB, D])

        scb = [bank(f"score_bank{n}") for n in range(SC_BANKS)]
        ob = bank("o_bank")
        ga = bank("ga_bank")
        gc = [bank("gc_bank0"), bank("gc_bank1")]

        w_in = sem("w_in")
        const_pool = sem("const_pool")
        const_dve = sem("const_dve")
        const_dma = sem("const_dma")
        mask_in = sem("mask_in")
        x_in = [sem("x_in0"), sem("x_in1")]
        tok_in = [sem("tok_in0"), sem("tok_in1")]
        stack_in = [sem("stack_in0"), sem("stack_in1")]
        max_in = [sem("max_in0"), sem("max_in1")]
        parts_out = sem("parts_out")
        out_done = [sem("out_done0"), sem("out_done1")]
        qk_ready = sem("qk_ready")
        qk_evac = sem("qk_evac")
        qk_hi, qk_rest, qk_mid, qk_low = (sem(n) for n in ("qk_hi", "qk_rest", "qk_mid", "qk_low"))
        v_ready = sem("v_ready")
        v_evac = sem("v_evac")
        v_hi, v_rest, v_mid, v_low = (sem(n) for n in ("v_hi", "v_rest", "v_mid", "v_low"))
        s_ready = sem("s_ready")
        s_done = sem("s_done")
        m_hi = sem("m_hi")
        m_low = sem("m_low")
        mt_ready = sem("mt_ready")
        mt_evac = sem("mt_evac")
        t_ready = sem("t_ready")
        t_done = sem("t_done")
        causal_done = sem("causal_done")
        ph_self = sem("ph_self")
        ph_cross = sem("ph_cross")
        pl_self = sem("pl_self")
        pl_cross = sem("pl_cross")
        pv_ready = sem("pv_ready")
        rden_ready = sem("rden_ready")
        pv_evac = sem("pv_evac")
        onorm_ready = sem("onorm_ready")
        att_ready = sem("att_ready")
        gc0_ready = sem("gc0_ready")
        gc0_evac = sem("gc0_evac")
        up_ready = sem("up_ready")
        gc1_ready = sem("gc1_ready")
        gc1_evac = sem("gc1_evac")
        xb_ready = sem("xb_ready")
        stat_ready = sem("stat_ready")
        mv_ready = sem("mv_ready")
        ve_ready = sem("ve_ready")
        rstd_ready = sem("rstd_ready")
        scaled_ready = sem("scaled_ready")
        n_ready = sem("n_ready")
        h_ready = sem("h_ready")
        nb_ready = sem("nb_ready")
        gelu_done = sem("gelu_done")
        relu_half = sem("relu_half")
        mask_float = sem("mask_float")
        nm_raw = sem("nm_raw")
        nm_ready = sem("nm_ready")
        p2_ready = sem("p2_ready")
        rden2_ready = sem("rden2_ready")
        x2_ready = sem("x2_ready")
        x2b_ready = sem("x2b_ready")
        o_ready = sem("o_ready")

        block = ctx.enter_context(nc.Block())

        def run(eng, body):
            def python_body(i):
                body(i, lambda n: Seq(n, n // 2, n % 2) if 0 <= n < B else None)

            for i in range(-2, 2):
                python_body(i)
            with eng.Fori(0, (B - 4) // 2) as j:
                for u in range(2):
                    body(None, lambda k, u=u: Seq(2 * j + (2 + u + k), j + (2 + u + k) // 2, (u + k) % 2))
            for i in range(B - 2, B + 1):
                python_body(i)

        def score_bank(s, k):
            return scb[(k + (S_BANKS + T_BANKS) * s.par) % SC_BANKS]

        def seqs(i, at):
            return [at(k if i is None else i + k) for k in (-1, 0, 1, 2)]

        @block.sync
        def _(sp):
            def load_x(s):
                sp.dma_start(xTs[s.par][:, :, :], xT[s.n]).then_inc(x_in[s.par], 16)
                sp.dma_start(cTs[s.par][:, :, :], ctxT[s.n]).then_inc(x_in[s.par], 16)

            sp.dma_start(mask_i[:, :], mask[:, :]).then_inc(mask_in, 16)
            sp.dma_start(xTs[0][:, :, :], xT[0]).then_inc(x_in[0], 16)
            sp.dma_start(cTs[0][:, :, :], ctxT[0]).then_inc(x_in[0], 16)
            loads = [(wqk[:, :, :, :, :], w_qk), (bqk[:, :, :], b_qk), (wv[:, :, :], w_v)]
            loads += [(t[:, b, :], v.partition_broadcast(P)) for t, v in ((bv2, b_v), (bo2, b_o), (bm2, b_m), (b22, b2))
                      for b in range(TB)]
            loads += [(wo[:, :, :], w_o), (wfc[:, :, :], w_fc), (bfc[:, :], b_fc), (wm[:, :, :], w_m),
                      (w1s[:, :, :], w1T), (b1s[:, :], b1), (w2s[:, :, :], w2T)]
            loads += [(t[:, :], v.partition_broadcast(P)) for t, v in ((g1s, g1), (be1s, be1), (g2s, g2), (be2s, be2))]
            for dst, src in loads:
                sp.dma_start(dst, src).then_inc(w_in, 16)
            assert len(loads) == N_LOADS
            load_x(Seq(1, 0, 1))
            sp.wait_ge(const_dve, 3)
            for p in range(2):
                for row, (q, k, c) in ((ROW_MASK, (1, 0, None)), (ROW_MASK + 1, (1, 0, None)),
                                       (ROW_SELF, (None, 1, 0)), (ROW_SELF + 1, (None, 1, 0)),
                                       (ROW_CROSS, (None, 0, 1)), (ROW_CROSS + 1, (None, 0, 1))):
                    for col, width, v in ((COL_Q, S, q), (COL_K, S, k), (COL_C, SE, c)):
                        if v is not None:
                            sp.dma_start(stack[p][row:row + 1, :, col:col + width],
                                         rows01[0:1, v, 0:width].rearrange("p (o c) -> p o c", o=1)
                                         .broadcast_to([1, H, width])).then_inc(const_dma, 16)
            sp.dma_start(mask_dram[:, :, :], mask_p[:, :, :]).then_inc(const_dma, 16)
            sp.wait_ge(const_dma, 16 * N_CONST_DMA)

            def stack_reads(s):
                wait(sp, t_ready, T_BANKS * (s.n - 1))
                st = stack[s.par]
                sp.dma_start(st[ROW_MASK:ROW_MASK + 2, :, COL_C:COLS],
                             mask_dram[s.n].rearrange("r (o c) -> r o c", o=1).broadcast_to([2, H, SE])
                             ).then_inc(stack_in[s.par], 16)
                sp.wait_ge(parts_out, 16 * (s.n + 1))
                src = parts_dram.rearrange("a (d h) g c -> (a d) (h g) c", d=HD)
                done = 0
                for rows, parts in ((0, 3), (3, 2), (5, 1)):
                    sp.dma_start(st[rows * HD:(rows + parts) * HD, :, COL_Q:COL_Q + S],
                                 src[0:parts * HD, :, COL_Q:COL_Q + S]).then_inc(stack_in[s.par], 16)
                    done += 1
                for slot, part in enumerate(K_PARTS):
                    sp.dma_start(st[slot * HD:(slot + 1) * HD, :, COL_K:COLS],
                                 src[part * HD:(part + 1) * HD, :, COL_K:COLS]).then_inc(stack_in[s.par], 16)
                    done += 1
                assert done == MAIN_READS

            def body(i, at):
                c, a, b, q = seqs(i, at)
                if q and (i is None or q.n >= 2):
                    sp.wait_ge(v_ready, 2 * (q.n - 1))
                    load_x(q)
                if a:
                    wait(sp, gc1_ready, 5 * (a.n - 1))
                    wait(sp, xb_ready, a.n - 1)
                    sp.dma_start(xt[a.par][:, :, :], x[a.n]).then_inc(tok_in[a.par], 16)
                    sp.dma_start(ct[a.par][:, :], ctx_t[a.n]).then_inc(tok_in[a.par], 16)
                    sp.dma_start(cTt[a.par][:, :, :], ctxT[a.n]).then_inc(tok_in[a.par], 16)
                if b:
                    sp.wait_ge(qk_hi, b.n + 1)
                    sp.wait_ge(qk_mid, b.n + 1)
                    sp.wait_ge(qk_low, b.n + 1)
                    if a:
                        sp.wait_ge(stack_in[a.par], 16 * (MAIN_READS + 1) * (a.half + 1))
                    sp.dma_start(parts_dram.rearrange("a p g c -> p a g c"), qk_p[:, :, :, :]).then_inc(parts_out, 16)
                if a:
                    sp.wait_ge(mt_evac, a.n + 1)
                    for r in range(4):
                        sp.dma_start(stack[a.par][ROW_SELF + r:ROW_SELF + r + 1, :, COL_Q:COL_Q + S],
                                     mT[r * H:(r + 1) * H, :]).then_inc(max_in[a.par], 16)
                if b:
                    stack_reads(b)
                if c:
                    sp.wait_ge(o_ready, c.n + 1)
                    sp.dma_start(out[c.n], o_sb[:, :, :]).then_inc(out_done[c.par], 16)

            run(sp, body)
            for p in range(2):
                sp.wait_ge(out_done[p], 16 * (B // 2))

        @block.tensor
        def _(pe):
            pe.wait_ge(w_in, 16 * N_LOADS)
            pe.wait_ge(const_pool, N_CONST_POOL)
            pe.wait_ge(const_dve, N_CONST_DVE)
            pe.wait_ge(const_dma, 16 * N_CONST_DMA)

            def numerators(s, q, banks):
                st = stack[s.par]
                if q == 0 and 0 in banks:
                    pe.wait_ge(max_in[s.par], 64 * (s.half + 1))
                for n in banks:
                    m = 5 * q + n
                    t = score_bank(s, S_BANKS + m)
                    if m < SC_BANKS:
                        pe.wait_ge(s_done, S_BANKS * s.n + S_BANKS - SC_BANKS + m + 1)
                    else:
                        pe.wait_ge(t_done, T_BANKS * s.n + m - SC_BANKS + 1)
                    heads = {0: (0, 1), 1: (2, 3), 2: (0, 1, 2, 3), 3: (0, 1), 4: (2, 3)}[n]
                    for e, h4 in enumerate(heads):
                        h = QH * q + h4
                        first, last = e == 0, e == len(heads) - 1
                        if n < 2:
                            mm = nc.tensor.matmul(t[:, e * S:(e + 1) * S], st[0:ROWS, h, COL_K:COL_K + P],
                                                  st[0:ROWS, h, COL_Q:COL_Q + S], start=first, stop=last,
                                                  skip_group_check=True)
                        elif n == 2:
                            mm = nc.tensor.matmul(t[:, e * P:(e + 1) * P], st[0:ROWS, h, COL_K + P:COL_K + S],
                                                  st[0:ROWS, h, COL_Q + P:COL_Q + S], start=first, stop=last,
                                                  skip_group_check=True)
                        else:
                            mm = nc.tensor.matmul(t[0:SE, e * S:(e + 1) * S], st[0:ROWS, h, COL_C:COLS],
                                                  st[0:ROWS, h, COL_Q:COL_Q + S], start=first, stop=last,
                                                  skip_group_check=True)
                    mm.then_inc(t_ready, 1)

            def products(s, q, qb):
                qn = 4 * s.n + q
                if qb == 0:
                    pe.wait_ge(pl_self, qn + 1)
                    pe.wait_ge(pl_cross, qn + 1)
                if q == 0 and qb == 0:
                    pe.wait_ge(v_hi, s.n + 1)
                    pe.wait_ge(v_mid, s.n + 1)
                    pe.wait_ge(v_low, s.n + 1)
                    pe.wait_ge(mt_evac, s.n + 1)
                else:
                    pe.wait_ge(pv_evac, 2 * qn + qb)
                first = True
                for h4 in range(QH):
                    for e in range(2):
                        u = 2 * h4 + e
                        if e == 0:
                            blocks = [(0, P, SELF0 + h4 * S + qb * P)]
                            if qb == 1:
                                blocks.append((1, P, SELF1 + h4 * P))
                        else:
                            blocks = [(2, SE, CROSS + h4 * S + qb * P)]
                        for blk, rows, col in blocks:
                            for w in (ph[q % 2], pl[q % 2]):
                                mm = nc.tensor.matmul(ob[:, u * HV:(u + 1) * HV], w[0:rows, col:col + P],
                                                      vp[0:rows, blk, QH * q + h4, :],
                                                      start=first, stop=False, skip_group_check=True)
                                first = False
                mm.then_inc(pv_ready, 1)

            def row_scores(s, banks):
                st = stack[s.par]
                R = ROW_SELF
                for m in banks:
                    if m == 0:
                        pe.wait_ge(stack_in[s.par], 16 * (MAIN_READS + 1) * (s.half + 1))
                    t = score_bank(s, m)
                    if m < SC_BANKS:
                        wait(pe, t_done, T_BANKS * (s.n - 1) + T_BANKS - SC_BANKS + m + 1)
                    else:
                        pe.wait_ge(s_done, S_BANKS * s.n + m - SC_BANKS + 1)
                    if m < 8:
                        o = t[:, :].rearrange("p (a c) -> p a c", a=2)
                        nc.tensor.matmul(o[:, :, P:S], identb[:, :], causal[:, 0:2, :], start=True, stop=False,
                                         skip_group_check=True)
                        for a in range(2):
                            h = 2 * m + a
                            mm = nc.tensor.matmul(o[:, a, :], st[0:R, h, COL_Q + P:COL_Q + S],
                                                  st[0:R, h, COL_K:COL_K + S], start=False, stop=a == 1,
                                                  skip_group_check=True)
                    elif m < 12:
                        o = t[:, :].rearrange("p (a c) -> p a c", a=4)
                        nc.tensor.matmul(o, identb[:, :], causal[:, :, :], start=True, stop=False,
                                         skip_group_check=True)
                        for a in range(4):
                            h = 4 * (m - 8) + a
                            mm = nc.tensor.matmul(o[:, a, :], st[0:R, h, COL_Q:COL_Q + P],
                                                  st[0:R, h, COL_K:COL_K + P], start=False, stop=a == 3,
                                                  skip_group_check=True)
                    else:
                        qb, run_ = divmod(m - 12, 3)
                        heads = range(CROSS_RUN * run_, min(CROSS_RUN * run_ + CROSS_RUN, H))
                        for a, h in enumerate(heads):
                            mm = nc.tensor.matmul(t[:, a * SE:(a + 1) * SE], st[0:R, h, COL_Q + qb * P:COL_Q + (qb + 1) * P],
                                                  st[0:R, h, COL_C:COLS], start=a == 0, stop=a == len(heads) - 1,
                                                  skip_group_check=True)
                    mm.then_inc(s_ready, 1)

            def max_transposes(s):
                pe.wait_ge(m_low, s.n + 1)
                wait(pe, pv_evac, 8 * s.n)
                for t in range(TB):
                    mm = nc.tensor.matmul(ob[0:4 * H, t * P:(t + 1) * P],
                                          mparts[:, t, :, :, :].rearrange("p a b h -> p (a b h)"), identb[:, :],
                                          start=t == 0, stop=True, skip_group_check=True)
                mm.then_inc(mt_ready, 1)

            def values(s, t):
                if t == 0:
                    pe.wait_ge(x_in[s.par], 32 * (s.half + 1))
                    pe.wait_ge(qk_evac, min(6 * s.n + 10, 6 * B) if isinstance(s.n, int) else 6 * s.n + 10)
                    wait(pe, gelu_done, 8 * (s.n - 1))
                if t == 2:
                    pe.wait_ge(v_evac, 2 * s.n + 1)
                for k in range(KC):
                    if t < 2:
                        mm = nc.tensor.matmul(ga[:, t * D:(t + 1) * D], xTs[s.par][:, k, t * P:(t + 1) * P], wv[:, k, :],
                                              start=t == 0 and k == 0, stop=k == KC - 1, skip_group_check=True)
                    else:
                        mm = nc.tensor.matmul(ga[0:SE, 0:D], cTs[s.par][:, k, :], wv[:, k, :], start=k == 0,
                                              stop=k == KC - 1)
                if t > 0:
                    mm.then_inc(v_ready, 1)

            def queries(s, step, g):
                if g == 0:
                    if step == 0:
                        pe.wait_ge(x_in[s.par], 32 * (s.half + 1))
                        wait(pe, qk_evac, 6 * s.n)
                        wait(pe, gelu_done, 8 * (s.n - 2))
                    else:
                        pe.wait_ge(qk_evac, 6 * s.n + 2 * step)
                        if step == 2:
                            wait(pe, v_evac, 2 * s.n)
                which, src, width = ((0, xTs, S), (1, xTs, S), (1, cTs, SE))[step]
                for k in range(KC):
                    mm = nc.tensor.matmul(ga[:, g * width:(g + 1) * width], wqk[:, k, which, g, :], src[s.par][:, k, :],
                                          start=g == 0 and k == 0, stop=k == KC - 1, skip_group_check=True)
                if g == GROUPS - 1:
                    mm.then_inc(qk_ready, 1)

            def into_gc1(s, use):
                wait(pe, gc1_evac, 5 * s.n + use)

            def transposes(src, dst):
                for k in range(KC):
                    for t in range(TB):
                        mm = nc.tensor.transpose(dst[:, k * S + t * P:k * S + (t + 1) * P],
                                                 src[:, t, k * P:(k + 1) * P], ident[:, :])
                return mm

            def by_token(dst, lhs, rhs, t):
                for k in range(KC):
                    mm = nc.tensor.matmul(dst[:, t * D:(t + 1) * D], lhs[:, k, t * P:(t + 1) * P], rhs[:, k, :],
                                          start=t == 0 and k == 0, stop=k == KC - 1, skip_group_check=True)
                return mm

            def up(s, j, e):
                dst = (gc[0], ga)[j % 2]
                if e == 0:
                    if j == 0:
                        pe.wait_ge(gc0_evac, 3 * s.n + 2)
                    elif j == 1:
                        pe.wait_ge(qk_evac, 6 * (min(s.n + 3, B) if isinstance(s.n, int) else s.n + 3))
                    else:
                        pe.wait_ge(gelu_done, 8 * s.n + 2 * (j - 2) + 2)
                f = 2 * j + e
                for k in range(KC):
                    mm = nc.tensor.matmul(dst[:, e * S:(e + 1) * S], wfc[:, k, f * P:(f + 1) * P], nT[:, k, :],
                                          start=e == 0 and k == 0, stop=k == KC - 1, skip_group_check=True)
                if e == 1:
                    mm.then_inc(up_ready, 1)

            def down(s, j, e):
                f = 2 * j + e
                if e == 0:
                    pe.wait_ge(gelu_done, 8 * s.n + 2 * j + 2)
                    if j == 0:
                        into_gc1(s, 1)
                for t in range(TB):
                    mm = nc.tensor.matmul(gc[1][:, t * D:(t + 1) * D], hid[:, f, t * P:(t + 1) * P], wm[:, f, :],
                                          start=f == 0 and t == 0, stop=f == FC - 1, skip_group_check=True)
                if f == FC - 1:
                    mm.then_inc(gc1_ready, 1)

            def scores2(s, t):
                if t == 0:
                    pe.wait_ge(gc0_evac, 3 * s.n + 3)
                    pe.wait_ge(tok_in[s.par], 48 * (s.half + 1))
                for k in range(KC):
                    mm = nc.tensor.matmul(gc[0][:, t * SE:(t + 1) * SE], hT[:, k, t * P:(t + 1) * P], cTt[s.par][:, k, :],
                                          start=t == 0 and k == 0, stop=k == KC - 1, skip_group_check=True)
                if t == TB - 1:
                    mm.then_inc(gc0_ready, 1)

            def relu_in(s, f):
                if f == 0:
                    pe.wait_ge(gc1_evac, 5 * s.n + 4)
                for k in range(KC):
                    mm = nc.tensor.matmul(gc[0][:, f * S:(f + 1) * S], w1s[:, k, f * P:(f + 1) * P], x2T[:, k, :],
                                          start=f == 0 and k == 0, stop=k == KC - 1, skip_group_check=True)
                if f == KC - 1:
                    mm.then_inc(gc0_ready, 1)

            def att_transposes(s):
                pe.wait_ge(att_ready, 4 * s.n + 4)
                wait(pe, relu_half, 2 * s.n)
                transposes(att[:, :, :, :].rearrange("p t h d -> p t (h d)"), gc[0]).then_inc(gc0_ready, 1)

            def output_projection(s):
                pe.wait_ge(gc0_evac, 3 * s.n + 1)
                into_gc1(s, 0)
                by_token(gc[1], attT, wo, 0)
                by_token(gc[1], attT, wo, 1).then_inc(gc1_ready, 1)

            def n_transposes(s):
                pe.wait_ge(n_ready, 2 * s.n + 2)
                transposes(n1, gc[0]).then_inc(gc0_ready, 1)

            def h_transposes(s):
                pe.wait_ge(h_ready, 2 * s.n + 2)
                pe.wait_ge(gelu_done, 8 * s.n + 6)
                transposes(h1, gc[0]).then_inc(gc0_ready, 1)

            def numerator2_transposes(s):
                pe.wait_ge(p2_ready, 2 * s.n + 2)
                into_gc1(s, 2)
                for t in range(TB):
                    mm = nc.tensor.transpose(gc[1][0:SE, t * P:(t + 1) * P], p2[:, t, :], ident[:, :])
                mm.then_inc(gc1_ready, 1)

            def products2(s):
                pe.wait_ge(gc1_evac, 5 * s.n + 3)
                for t in range(TB):
                    mm = nc.tensor.matmul(gc[0][:, t * D:(t + 1) * D], p2T[:, t * P:(t + 1) * P], ct[s.par][:, :],
                                          start=t == 0, stop=True, skip_group_check=True)
                mm.then_inc(gc0_ready, 1)

            def x2_transposes(s):
                pe.wait_ge(x2_ready, 2 * s.n + 2)
                into_gc1(s, 3)
                transposes(x2, gc[1]).then_inc(gc1_ready, 1)

            def relu_out(s, t):
                if t == 0:
                    pe.wait_ge(relu_half, 2 * s.n + 2)
                    into_gc1(s, 4)
                mm = by_token(gc[1], r2T, w2s, t)
                if t == TB - 1:
                    mm.then_inc(gc1_ready, 1)

            def body(i, at):
                c, a, b, q = seqs(i, at)

                def do(s, step, *args):
                    if s:
                        step(s, *args)

                do(a, row_scores, (0, 1, 2))
                do(c, att_transposes)
                do(a, row_scores, (3, 4))
                do(c, output_projection)
                do(b, queries, 2, 0)
                do(b, queries, 2, 1)
                do(a, row_scores, (5, 6, 7, 8))
                do(c, n_transposes)
                do(a, row_scores, (9, 10))
                do(c, up, 0, 0)
                do(a, row_scores, (11, 12))
                do(c, up, 0, 1)
                do(a, row_scores, (13,))
                do(c, up, 1, 0)
                do(a, row_scores, (14, 15))
                do(c, up, 1, 1)
                do(a, row_scores, (16,))
                do(c, down, 0, 0)
                do(a, row_scores, (17,))
                do(c, down, 0, 1)
                do(c, up, 2, 0)
                do(a, max_transposes)
                do(c, up, 2, 1)
                do(c, down, 1, 0)
                do(c, down, 1, 1)
                do(c, up, 3, 0)
                do(c, up, 3, 1)
                do(c, down, 2, 0)
                do(c, down, 2, 1)
                do(a, numerators, 0, (0,))
                do(c, down, 3, 0)
                do(a, numerators, 0, (1, 2))
                do(c, down, 3, 1)
                do(a, numerators, 0, (3, 4))
                do(q, queries, 0, 0)
                do(a, numerators, 1, (0,))
                do(q, queries, 0, 1)
                do(a, numerators, 1, (1,))
                do(q, queries, 1, 0)
                do(a, numerators, 1, (2,))
                do(q, queries, 1, 1)
                do(a, numerators, 1, (3,))
                do(c, h_transposes)
                do(a, numerators, 1, (4,))
                do(a, products, 0, 0)
                do(a, numerators, 2, (0,))
                do(c, scores2, 0)
                do(c, scores2, 1)
                do(a, numerators, 2, (1,))
                do(a, products, 0, 1)
                do(a, numerators, 2, (2,))
                do(b, values, 0)
                do(a, numerators, 2, (3,))
                do(a, products, 1, 0)
                do(c, numerator2_transposes)
                do(a, numerators, 2, (4,))
                do(b, values, 1)
                do(a, numerators, 3, (0,))
                do(a, products, 1, 1)
                do(a, numerators, 3, (1,))
                do(c, products2)
                do(a, numerators, 3, (2, 3))
                do(a, products, 2, 0)
                do(c, x2_transposes)
                do(a, numerators, 3, (4,))
                do(b, values, 2)
                do(a, products, 2, 1)
                do(c, relu_in, 0)
                do(c, relu_in, 1)
                do(a, products, 3, 0)
                do(c, relu_out, 0)
                do(c, relu_out, 1)
                do(a, products, 3, 1)

            run(pe, body)

        @block.scalar
        def _(act):
            act.wait_ge(w_in, 16 * N_LOADS)

            def exps(s, q, banks):
                qn = 4 * s.n + q
                if 0 in banks:
                    wait(act, pl_self, qn - 1)
                    wait(act, pl_cross, qn - 1)
                dst = pf[q % 2]
                places = ((P, SELF0), (P, SELF0 + 512), (P, SELF1), (SE, CROSS), (SE, CROSS + 512))
                for n in banks:
                    rows, col = places[n]
                    m = 5 * q + n
                    act.wait_ge(t_ready, T_BANKS * s.n + m + 1)
                    nc.scalar.activation(dst[0:rows, col:col + 512], score_bank(s, S_BANKS + m)[0:rows, :], ACT.Exp,
                                         scale=HD ** -0.5).then_inc(t_done, 1)

            def high_cross(s, q):
                wait(act, pv_ready, 2 * (4 * s.n + q - 1))
                act.wait_ge(t_done, T_BANKS * s.n + 5 * q + 5)
                nc.scalar.activation(ph[q % 2][0:SE, CROSS:QUAD_COLS], pf[q % 2][0:SE, CROSS:QUAD_COLS],
                                     ACT.Copy).then_inc(ph_cross, 1)

            def queries_out(s, step):
                if step == 0:
                    wait(act, qk_hi, s.n)
                    wait(act, qk_rest, s.n)
                which, col, width = ((0, COL_Q, S), (1, COL_K, S), (1, COL_C, SE))[step]
                act.wait_ge(qk_ready, 3 * s.n + step + 1)
                for g in range(GROUPS):
                    nc.scalar.activation(qk_f[:, g, col:col + width], ga[:, g * width:(g + 1) * width], ACT.Identity,
                                         bias=bqk[:, which, g:g + 1]).then_inc(qk_evac, 1)

            def gelu(s, j):
                act.wait_ge(up_ready, 4 * s.n + j + 1)
                if j == 0:
                    wait(act, gc1_ready, 5 * (s.n - 1) + 2)
                for e in range(2):
                    f = 2 * j + e
                    nc.scalar.activation(hid[:, f, :], (gc[0], ga)[j % 2][:, e * S:(e + 1) * S], ACT.Gelu_apprx_tanh,
                                         bias=bfc[:, f:f + 1]).then_inc(gelu_done, 1)

            def from_gc0(s, use, dst, src):
                act.wait_ge(gc0_ready, 6 * s.n + use)
                nc.scalar.activation(dst, src, ACT.Copy).then_inc(gc0_evac, 1)

            def from_gc1(s, use, dst, src):
                act.wait_ge(gc1_ready, 5 * s.n + use)
                nc.scalar.activation(dst, src, ACT.Copy).then_inc(gc1_evac, 1)

            def flat(t):
                return t[:, :, :].rearrange("p k s -> p (k s)")

            def body(i, at):
                c, a, b, q = seqs(i, at)
                if c:
                    from_gc0(c, 1, flat(attT), gc[0][:, :])
                if b:
                    queries_out(b, 2)
                if c:
                    from_gc0(c, 2, flat(nT), gc[0][:, :])
                    gelu(c, 0)
                    gelu(c, 1)
                if a:
                    act.wait_ge(mt_ready, a.n + 1)
                    wait(act, max_in[1 - a.par], 64 * (a.half + a.par))
                    nc.scalar.activation(mT[:, :], ob[0:4 * H, 0:S], ACT.Copy).then_inc(mt_evac, 1)
                if c:
                    gelu(c, 2)
                    gelu(c, 3)
                if a:
                    exps(a, 0, range(5))
                    exps(a, 1, (0,))
                if q:
                    queries_out(q, 0)
                if a:
                    exps(a, 1, (1,))
                    high_cross(a, 0)
                    exps(a, 1, (2,))
                if q:
                    queries_out(q, 1)
                if a:
                    exps(a, 1, (3,))
                if c:
                    from_gc0(c, 3, flat(hT), gc[0][:, :])
                if a:
                    exps(a, 1, (4,))
                    high_cross(a, 1)
                    exps(a, 2, (0, 1, 2))
                if c:
                    act.wait_ge(nm_ready, c.n + 1)
                    wait(act, gc1_ready, 5 * (c.n - 1) + 3)
                    wait(act, rden2_ready, c.n)
                    for t in range(TB):
                        nc.scalar.activation(p2[:, t, :], gc[0][:, t * SE:(t + 1) * SE], ACT.Exp, scale=D ** -0.5,
                                             bias=nms[:, t:t + 1], accum_out=den2[:, t:t + 1]).then_inc(p2_ready, 1)
                if a:
                    exps(a, 2, (3,))
                if c:
                    from_gc1(c, 3, p2T[:, :], gc[1][0:SE, 0:S])
                if a:
                    exps(a, 2, (4,))
                    high_cross(a, 2)
                    exps(a, 3, (0, 1, 2, 3))
                if c:
                    from_gc1(c, 4, flat(x2T), gc[1][:, :])
                if a:
                    exps(a, 3, (4,))
                    high_cross(a, 3)
                if c:
                    act.wait_ge(gc0_ready, 6 * c.n + 6)
                    for f in range(KC):
                        nc.scalar.activation(r2T[:, f, :], gc[0][:, f * S:(f + 1) * S], ACT.Relu,
                                             bias=b1s[:, f:f + 1]).then_inc(relu_half, 1)

            run(act, body)

        @block.vector
        def _(dve):
            v = nc.vector
            v.memset(rows01[:, 0, :], 0.0).then_inc(const_dve, 1)
            v.memset(rows01[:, 1, :], 1.0).then_inc(const_dve, 1)
            dve.wait_ge(mask_in, 16)
            v.tensor_copy(mask_f[:, :], mask_i[:, :]).then_inc(mask_float, 1)
            dve.wait_ge(mask_float, 1)
            v.tensor_scalar(mask_p[:, 0, :], mask_f[:, :], -99840.0 * HD ** 0.5, None, ALU.mult)
            v.tensor_scalar(mask_p[:, 1, :], mask_f[:, :], (NEG + 99840.0) * HD ** 0.5, None, ALU.mult).then_inc(const_dve, 1)
            v.memset(half_pow[:, :], -0.5).then_inc(const_dve, 1)
            v.memset(vp[:, :, :, V_PARTS * HD:HV], 1.0).then_inc(const_dve, 1)
            v.memset(v_f[:, 2, :], 0.0).then_inc(const_dve, 1)
            dve.wait_ge(w_in, 16 * N_LOADS)
            v.tensor_scalar(wo[:, :, :], wo[:, :, :], 0.5, None, ALU.mult).then_inc(const_dve, 1)
            dve.wait_ge(const_dve, N_CONST_DVE)
            dve.wait_ge(const_pool, N_CONST_POOL)

            def heads(t, blk=slice(0, 3)):
                return t[:, blk, :].rearrange("p b (h d) -> p (b h) d", d=HD)

            def part(k):
                return vp[:, :, :, k * HD:(k + 1) * HD].rearrange("p b h d -> p (b h) d")

            def split_self(s, q):
                qn = 4 * s.n + q
                wait(dve, pv_ready, 2 * (qn - 1))
                dve.wait_ge(causal_done, 2 * qn + 2)
                v.tensor_copy(ph[q % 2][:, 0:CROSS], pf[q % 2][:, 0:CROSS]).then_inc(ph_self, 1)
                dve.wait_ge(ph_self, qn + 1)
                v.tensor_tensor(pl[q % 2][:, 0:CROSS], pf[q % 2][:, 0:CROSS], ph[q % 2][:, 0:CROSS],
                                ALU.subtract).then_inc(pl_self, 1)

            def add_parts(s, q, qb):
                n = 2 * (4 * s.n + q) + qb
                units = slice(qb * HALF_UNITS, (qb + 1) * HALF_UNITS)
                o = ob[:, 0:HALF_UNITS * HV].rearrange("p (u c) -> p u c", c=HV)
                dve.wait_ge(pv_ready, n + 1)
                if qb == 0:
                    wait(dve, onorm_ready, 4 * s.n + q)
                v.reciprocal(rden[:, units], o[:, :, V_PARTS * HD]).then_inc(rden_ready, 1)
                v.tensor_reduce(osum[:, units, :], o[:, :, 0:V_PARTS * HD].rearrange("p u (k d) -> p u d k", d=HD),
                                AX_X, ALU.add).then_inc(pv_evac, 1)

            def norm(s, q):
                qn = 4 * s.n + q
                dve.wait_ge(rden_ready, 2 * qn + 2)
                dve.wait_ge(pv_evac, 2 * qn + 2)
                wait(dve, att_ready, qn)
                r = rden[:, :]
                rb = bass.AP(r.tensor, r.offset, [[UNITS, P], [1, UNITS], [0, HD]])
                v.tensor_tensor(onorm[:, :, :], osum[:, :, :], rb, ALU.mult).then_inc(onorm_ready, 1)
                dve.wait_ge(onorm_ready, qn + 1)
                if q == 0:
                    wait(dve, gc0_ready, 6 * (s.n - 1) + 1)
                on = onorm[:, :, :].rearrange("p (t h a) d -> p a t h d", t=TB, a=2)
                for t in range(TB):
                    ins = v.tensor_tensor(att[:, t, QH * q:QH * q + QH, :], on[:, 0, t], on[:, 1, t], ALU.add)
                ins.then_inc(att_ready, 1)

            def row_max(s, banks):
                for m in banks:
                    dve.wait_ge(s_ready, S_BANKS * s.n + m + 1)
                    if m == 0:
                        wait(dve, m_low, s.n)
                    t = score_bank(s, m)
                    if m < 8:
                        src, dst = t[:, :].rearrange("p (a c) -> p a c", a=2), mx[:, 1, 0, 2 * m:2 * m + 2]
                    elif m < 12:
                        src, dst = t[:, :].rearrange("p (a c) -> p a c", a=4), mx[:, 0, 0, 4 * (m - 8):4 * (m - 7)]
                    else:
                        qb, run_ = divmod(m - 12, 3)
                        h0, h1_ = CROSS_RUN * run_, min(CROSS_RUN * run_ + CROSS_RUN, H)
                        src = t[:, 0:(h1_ - h0) * SE].rearrange("p (a c) -> p a c", c=SE)
                        dst = mx[:, qb, 1, h0:h1_]
                    v.tensor_reduce(dst, src, AX_X, ALU.max, negate=True).then_inc(s_done, 1)

            def max_parts(s):
                dve.wait_ge(s_done, S_BANKS * (s.n + 1))
                wait(dve, mt_ready, s.n)
                for t in range(TB):
                    ins = v.tensor_copy(mparts[:, t, :, 0, :], mx[:, t, :, :])
                ins.then_inc(m_hi, 1)
                dve.wait_ge(m_hi, s.n + 1)
                for t in range(TB):
                    ins = v.tensor_tensor(mparts[:, t, :, 1, :], mx[:, t, :, :], mparts[:, t, :, 0, :], ALU.subtract)
                ins.then_inc(m_low, 1)

            def layer_stats(s, src, ln):
                for t in range(TB):
                    v.bn_stats(stats[:, t, :], src[:, t, :]).then_inc(stat_ready, 1)
                dve.wait_ge(stat_ready, 4 * s.n + 2 * ln + 2)
                v.memset(tick[:, 3:4], 0.0)
                for t in range(TB):
                    v.bn_aggr(mv[:, t, :], stats[:, t, :]).then_inc(mv_ready, 1)
                dve.wait_ge(mv_ready, 4 * s.n + 2 * ln + 2)
                v.tensor_scalar(ve[:, :], mv[:, :, 1], EPS, None, ALU.add).then_inc(ve_ready, 1)

            def layer_scale(s, src, gamma, ln):
                for t in range(TB):
                    v.scalar_tensor_tensor(scaled[:, t, :], src[:, t, :], mv[:, t, 0:1], gamma[:, :],
                                           ALU.subtract, ALU.mult).then_inc(scaled_ready, 1)

            def layer_out(s, dst, beta, ln, done):
                dve.wait_ge(scaled_ready, 4 * s.n + 2 * ln + 2)
                dve.wait_ge(rstd_ready, 2 * s.n + ln + 1)
                for t in range(TB):
                    v.scalar_tensor_tensor(dst[:, t, :], scaled[:, t, :], rstd[:, t:t + 1], beta[:, :],
                                           ALU.mult, ALU.add).then_inc(done, 1)

            def both(t):
                return t[:, :, :].rearrange("p t d -> p (t d)")

            def body(i, at):
                c, a, b, q = seqs(i, at)
                if a:
                    row_max(a, range(0, 5))
                if c:
                    dve.wait_ge(gc1_ready, 5 * c.n + 1)
                    dve.wait_ge(xb_ready, c.n + 1)
                    v.tensor_tensor(both(y), gc[1][:, :], both(xb), ALU.add).then_inc(gc1_evac, 1)
                    dve.wait_ge(gc1_evac, 5 * c.n + 1)
                    layer_stats(c, y, 0)
                    dve.wait_ge(mv_ready, 4 * c.n + 2)
                    layer_scale(c, y, g1s, 0)
                    layer_out(c, n1, be1s, 0, n_ready)
                if a:
                    row_max(a, range(5, 9))
                    dve.wait_ge(v_evac, 2 * a.n + 2)
                    wait(dve, pv_ready, 8 * a.n)
                    v.tensor_copy(part(0), heads(v_f)).then_inc(v_hi, 1)
                    row_max(a, range(9, 13))
                if b:
                    dve.wait_ge(qk_evac, 6 * (b.n + 1))
                    wait(dve, parts_out, 16 * b.n)
                    v.tensor_copy(qk_p[:, 0, :, :], qk_f[:, :, :]).then_inc(qk_hi, 1)
                if a:
                    row_max(a, range(13, S_BANKS))
                    max_parts(a)
                    dve.wait_ge(v_rest, a.n + 1)
                    v.tensor_copy(part(1), heads(v_r)).then_inc(v_mid, 1)
                if b:
                    dve.wait_ge(qk_rest, b.n + 1)
                    v.tensor_copy(qk_p[:, 1, :, :], qk_r[:, :, :]).then_inc(qk_mid, 1)
                if c:
                    dve.wait_ge(gc1_ready, 5 * c.n + 2)
                    dve.wait_ge(nb_ready, c.n + 1)
                    v.tensor_tensor(both(z), gc[1][:, :], both(nb), ALU.add).then_inc(gc1_evac, 1)
                    dve.wait_ge(gc1_evac, 5 * c.n + 2)
                    layer_stats(c, z, 1)
                    dve.wait_ge(mv_ready, 4 * c.n + 4)
                    layer_scale(c, z, g2s, 1)
                    layer_out(c, h1, be2s, 1, h_ready)
                if a:
                    split_self(a, 0)
                    split_self(a, 1)
                if c:
                    dve.wait_ge(gc0_ready, 6 * c.n + 4)
                    v.tensor_reduce(nm[:, :], gc[0][:, 0:TB * SE].rearrange("p (t c) -> p t c", t=TB), AX_X, ALU.max,
                                    negate=True).then_inc(nm_raw, 1)
                    dve.wait_ge(nm_raw, c.n + 1)
                    v.tensor_scalar(nms[:, :], nm[:, :], D ** -0.5, None, ALU.mult).then_inc(nm_ready, 1)
                if a:
                    add_parts(a, 0, 0)
                    add_parts(a, 0, 1)
                    norm(a, 0)
                    add_parts(a, 1, 0)
                    split_self(a, 2)
                if b:
                    dve.wait_ge(v_ready, 2 * b.n + 1)
                    wait(dve, v_rest, b.n)
                    wait(dve, v_hi, b.n)
                    v.tensor_tensor(both(v_f[:, 0:2, :]), ga[:, :], both(bv2), ALU.add).then_inc(v_evac, 1)
                if a:
                    add_parts(a, 1, 1)
                    norm(a, 1)
                if c:
                    dve.wait_ge(p2_ready, 2 * c.n + 2)
                    v.reciprocal(rden2[:, :], den2[:, :]).then_inc(rden2_ready, 1)
                    dve.wait_ge(rden2_ready, c.n + 1)
                    dve.wait_ge(gc0_ready, 6 * c.n + 5)
                    for t in range(TB):
                        v.scalar_tensor_tensor(x2[:, t, :], gc[0][:, t * D:(t + 1) * D], rden2[:, t:t + 1], h1[:, t, :],
                                               ALU.mult, ALU.add).then_inc(x2_ready, 1)
                if a:
                    add_parts(a, 2, 0)
                    split_self(a, 3)
                if b:
                    dve.wait_ge(v_ready, 2 * b.n + 2)
                    v.tensor_tensor(v_f[0:SE, 2, :], ga[0:SE, 0:D], bv2[0:SE, 0, :], ALU.add).then_inc(v_evac, 1)
                if a:
                    add_parts(a, 2, 1)
                    norm(a, 2)
                    add_parts(a, 3, 0)
                if c:
                    dve.wait_ge(gc1_ready, 5 * c.n + 5)
                    dve.wait_ge(x2b_ready, c.n + 1)
                    wait(dve, out_done[1 - c.par], 16 * (c.half + c.par))
                    v.tensor_tensor(both(o_sb), gc[1][:, :], both(x2b), ALU.add).then_inc(gc1_evac, 1)
                    dve.wait_ge(gc1_evac, 5 * c.n + 5)
                    v.memset(tick[:, 3:4], 0.0).then_inc(o_ready, 1)
                if a:
                    add_parts(a, 3, 1)
                    norm(a, 3)

            run(dve, body)

        @block.gpsimd
        def _(pool):
            g = nc.gpsimd
            g.memset(ident[:, :], 0.0).then_inc(const_pool, 1)
            g.memset(identb[:, :], 0.0).then_inc(const_pool, 1)
            g.memset(causal[:, :, :], -1e30).then_inc(const_pool, 1)
            g.memset(ptick[:, :], 0.0).then_inc(const_pool, 1)
            pool.wait_ge(const_pool, 4)
            for m in (ident, identb):
                g.affine_select(out=m[:, :], in_=m[:, :], compare_op=ALU.not_equal, fill=1.0, base=0,
                                pattern=[[-1, P]], channel_multiplier=1).then_inc(const_pool, 1)
            g.affine_select(out=causal[:, :, :], in_=causal[:, :, :], compare_op=ALU.is_gt, fill=0.0, base=0,
                            pattern=[[0, 4], [1, P]], channel_multiplier=-1).then_inc(const_pool, 1)
            pool.wait_ge(const_dve, N_CONST_DVE)
            pool.wait_ge(w_in, 16 * N_LOADS)
            pool.wait_ge(const_pool, N_CONST_POOL)

            def carry(q):
                g.tensor_tensor(ptick[:, 2 + q:3 + q], ptick[:, 0:1], ptick[:, 1:2], ALU.add)

            def clear_masked(s, q):
                pool.wait_ge(t_done, T_BANKS * s.n + 5 * q + 3)
                carry(q)
                d0 = pf[q % 2][:, SELF0:SELF1].rearrange("p (h c) -> p h c", h=QH)[:, :, 0:P]
                d1 = pf[q % 2][:, SELF1:CROSS].rearrange("p (h c) -> p h c", h=QH)
                for d in (d0, d1):
                    g.affine_select(out=d, in_=d, compare_op=ALU.is_ge, fill=0.0, base=0,
                                    pattern=[[0, QH], [1, P]], channel_multiplier=-1).then_inc(causal_done, 1)

            def low_cross(s, q):
                qn = 4 * s.n + q
                pool.wait_ge(ph_cross, qn + 1)
                g.tensor_tensor(pl[q % 2][0:SE, CROSS:QUAD_COLS], pf[q % 2][0:SE, CROSS:QUAD_COLS],
                                ph[q % 2][0:SE, CROSS:QUAD_COLS], ALU.subtract).then_inc(pl_cross, 1)

            def heads(t):
                return t[:, :, :].rearrange("p b (h d) -> p (b h) d", d=HD)

            def part(k):
                return vp[:, :, :, k * HD:(k + 1) * HD].rearrange("p b h d -> p (b h) d")

            def body(i, at):
                c, a, b, q = seqs(i, at)
                if c:
                    pool.wait_ge(ve_ready, 2 * c.n + 1)
                    g.tensor_tensor(rstd[:, :], ve[:, :], half_pow[:, :], ALU.pow).then_inc(rstd_ready, 1)
                if a:
                    pool.wait_ge(v_hi, a.n + 1)
                    wait(pool, v_mid, a.n)
                    g.tensor_tensor(heads(v_r), heads(v_f), part(0), ALU.subtract).then_inc(v_rest, 1)
                if b:
                    pool.wait_ge(qk_hi, b.n + 1)
                    g.tensor_tensor(qk_r[:, :, :], qk_f[:, :, :], qk_p[:, 0, :, :], ALU.subtract).then_inc(qk_rest, 1)
                if c:
                    pool.wait_ge(n_ready, 2 * c.n + 2)
                    wait(pool, gc1_evac, 5 * (c.n - 1) + 2)
                    g.tensor_tensor(nb[:, :, :], n1[:, :, :], bm2[:, :, :], ALU.add).then_inc(nb_ready, 1)
                if a:
                    pool.wait_ge(v_mid, a.n + 1)
                    g.tensor_tensor(part(2), heads(v_r), part(1), ALU.subtract).then_inc(v_low, 1)
                if b:
                    pool.wait_ge(qk_mid, b.n + 1)
                    g.tensor_tensor(qk_p[:, 2, :, :], qk_r[:, :, :], qk_p[:, 1, :, :], ALU.subtract).then_inc(qk_low, 1)
                if a:
                    clear_masked(a, 0)
                if c:
                    pool.wait_ge(ve_ready, 2 * c.n + 2)
                    g.tensor_tensor(rstd[:, :], ve[:, :], half_pow[:, :], ALU.pow).then_inc(rstd_ready, 1)
                if a:
                    low_cross(a, 0)
                    clear_masked(a, 1)
                    low_cross(a, 1)
                    clear_masked(a, 2)
                    low_cross(a, 2)
                if c:
                    pool.wait_ge(x2_ready, 2 * c.n + 2)
                    wait(pool, gc1_evac, 5 * c.n)
                    g.tensor_tensor(x2b[:, :, :], x2[:, :, :], b22[:, :, :], ALU.add).then_inc(x2b_ready, 1)
                if a:
                    clear_masked(a, 3)
                    low_cross(a, 3)
                    pool.wait_ge(tok_in[a.par], 48 * (a.half + 1))
                    wait(pool, gc1_evac, 5 * (a.n - 1) + 1)
                    g.tensor_tensor(xb[:, :, :], xt[a.par][:, :, :], bo2[:, :, :], ALU.add).then_inc(xb_ready, 1)

            run(pool, body)


N_LOADS = 22
N_CONST_DMA = 2 * (2 * 2 + 4 * 2) + 1
N_CONST_POOL = 7
N_CONST_DVE = 7


def kernel(x, ctx_1024, mask_BxS2_ik0, L0_xattn_w_attn, L0_xattn_b_attn, L0_xattn_w_oproj, L0_xattn_b_oproj,
           L0_xattn_w_fc, L0_xattn_b_fc, L0_xattn_w_mproj, L0_xattn_b_mproj, L0_xattn_ln1_g, L0_xattn_ln1_b,
           L0_xattn_ln2_g, L0_xattn_ln2_b, L1_xattn_W1, L1_xattn_b1, L1_xattn_W2, L1_xattn_b2):
    import concourse.bacc as bacc
    from concourse.bass_utils import run_bass_kernel_spmd

    def chunks(w):
        w = np.asarray(w)
        return w.reshape(-1, P, w.shape[1]).transpose(1, 0, 2)

    def columns(b):
        return np.asarray(b).reshape(-1, P).T

    def head_groups(w):
        w = np.asarray(w)
        return w.reshape(*w.shape[:-1], GH, GROUPS, HD).swapaxes(-3, -2).swapaxes(-1, -2).reshape(
            *w.shape[:-1], GROUPS, P)

    xs, cs, wa, ba = (np.asarray(t) for t in (x, ctx_1024, L0_xattn_w_attn, L0_xattn_b_attn))
    w_qk = np.stack([head_groups(wa[:, :D]), head_groups(wa[:, D:2 * D])], 1)
    b_qk = np.stack([head_groups(ba[:D]), head_groups(ba[D:2 * D])], 0)
    arrays = {
        "x_tok": xs.reshape(B, TB, P, D).transpose(0, 2, 1, 3),
        "x_chan": xs.transpose(0, 2, 1).reshape(B, KC, P, S).transpose(0, 2, 1, 3),
        "ctx_tok": cs,
        "ctx_chan": cs.transpose(0, 2, 1).reshape(B, KC, P, SE).transpose(0, 2, 1, 3),
        "mask": np.asarray(mask_BxS2_ik0),
        "w_qk": w_qk.reshape(KC, P, 2, GROUPS, P).transpose(1, 0, 2, 3, 4),
        "b_qk": b_qk.transpose(2, 0, 1),
        "w_v": chunks(wa[:, 2 * D:]),
        "b_v": ba[2 * D:],
        "w_o": chunks(L0_xattn_w_oproj),
        "b_o": L0_xattn_b_oproj,
        "w_fc": chunks(L0_xattn_w_fc),
        "b_fc": columns(L0_xattn_b_fc),
        "w_m": chunks(L0_xattn_w_mproj),
        "b_m": L0_xattn_b_mproj,
        "g1": L0_xattn_ln1_g,
        "be1": L0_xattn_ln1_b,
        "g2": L0_xattn_ln2_g,
        "be2": L0_xattn_ln2_b,
        "w1T": chunks(np.asarray(L1_xattn_W1).T),
        "b1": columns(L1_xattn_b1),
        "w2T": chunks(np.asarray(L1_xattn_W2).T),
        "b2": L1_xattn_b2,
    }
    arrays = {f"in_{k}": np.ascontiguousarray(np.asarray(v)) for k, v in arrays.items()}
    nc = bacc.Bacc("TRN2", target_bir_lowering=False, num_devices=1)
    args = [nc.dram_tensor(k, v.shape, mybir.dt.from_np(v.dtype), kind="ExternalInput").ap() for k, v in arrays.items()]
    args.append(nc.dram_tensor("out_0", (B, P, TB, D), F32, kind="ExternalOutput").ap())
    build(nc, *args)
    got = run_bass_kernel_spmd(nc, [arrays], core_ids=[0]).results[0]["out_0"]
    return np.ascontiguousarray(got.transpose(0, 2, 1, 3).reshape(B, S, D))
```

```python
from contextlib import ExitStack

import numpy as np

import concourse.bass as bass
from concourse import mybir

ALU = mybir.AluOpType
ACT = mybir.ActivationFunctionType
F32 = mybir.dt.float32
BF16 = mybir.dt.bfloat16
F16 = mybir.dt.float16
I32 = mybir.dt.int32
AX_X = mybir.AxisListType.X

P = 128
B, S, D = 32, 256, 256
SE = 77
H, HD = 16, 16
F = 4 * D
KC = D // P
TB = S // P
FC = F // P
QH = 4
QUADS = H // QH
EPS = 1e-5
NEG = -100000.0

Q_PARTS = (0, 1, 2, 0, 1, 0)
K_PARTS = (0, 0, 0, 1, 1, 2)
SLOTS = len(Q_PARTS)
ROW_MASK = SLOTS * HD
ROW_SELF = ROW_MASK + 2
ROW_CROSS = ROW_SELF + 2
ROWS = ROW_CROSS + 2
COL_Q, COL_K, COL_C = 0, S, 2 * S
COLS = 2 * S + SE
GROUPS = 2
GH = H // GROUPS

SELF0, SELF1, CROSS = 0, QH * S, QH * S + QH * P
QUAD_COLS = CROSS + QH * S
V_PARTS = 3
HV = V_PARTS * HD + 1
HALF_UNITS = QH * 2
UNITS = TB * HALF_UNITS
CROSS_RUN = 6
S_BANKS = 8 + 4 + 2 * 3
T_BANKS = 5 * QUADS
SC_BANKS = 3
MAIN_READS = 9


class Seq:

    def __init__(self, n, half, par):
        self.n, self.half, self.par = n, half, par


def wait(eng, sem, value):
    if not (isinstance(value, int) and value <= 0):
        eng.wait_ge(sem, value)


def build(nc, x, xT, ctx_t, ctxT, mask, w_qk, b_qk, w_v, b_v, w_o, b_o, w_fc, b_fc, w_m, b_m,
          g1, be1, g2, be2, w1T, b1, w2T, b2, out):
    ctx = ExitStack()
    with ctx:
        def sb(name, shape, dt=F32):
            return ctx.enter_context(nc.sbuf_tensor(name, shape, dt))

        def bank(name):
            return ctx.enter_context(nc.psum_tensor(name, [P, 512], F32))

        def sem(name):
            return ctx.enter_context(nc.semaphore(name))

        parts_dram = nc.dram_tensor("parts_scratch", (3, P, GROUPS, COLS), BF16, kind="Internal").ap()
        mask_dram = nc.dram_tensor("mask_scratch", (B, 2, SE), BF16, kind="Internal").ap()

        wqk = sb("wqk", [P, KC, 2, GROUPS, P])
        bqk = sb("bqk", [P, 2, GROUPS])
        wv = sb("wv", [P, KC, D])
        wo = sb("wo", [P, KC, D])
        wfc = sb("wfc", [P, KC, F])
        bfc = sb("bfc", [P, FC])
        wm = sb("wm", [P, FC, D])
        w1s = sb("w1s", [P, KC, D])
        b1s = sb("b1s", [P, KC])
        w2s = sb("w2s", [P, KC, D])
        bvs, bos, bms, b2s = (sb(n, [P, D]) for n in ("bvs", "bos", "bms", "b2s"))
        g1s, be1s, g2s, be2s = (sb(n, [P, D]) for n in ("g1s", "be1s", "g2s", "be2s"))
        ident = sb("ident", [P, P])
        identb = sb("identb", [P, P], BF16)
        causal = sb("causal", [P, 4, P], BF16)
        half_pow = sb("half_pow", [P, TB])
        ones = sb("ones", [2, S], BF16)
        mask_i = sb("mask_i", [B, SE], I32)
        mask_f = sb("mask_f", [B, SE])
        mask_p = sb("mask_p", [B, 2, SE], BF16)
        ptick = sb("ptick", [P, 2 + QUADS])
        tick = sb("tick", [P, 4])

        xTs = [sb(f"xTs{p}", [P, KC, S]) for p in range(2)]
        cTs = [sb(f"cTs{p}", [P, KC, SE]) for p in range(2)]
        xt = [sb(f"xt{p}", [P, TB, D]) for p in range(2)]
        ct = [sb(f"ct{p}", [SE, D]) for p in range(2)]
        cTt = [sb(f"cTt{p}", [P, KC, SE]) for p in range(2)]
        stack = [sb(f"stack{p}", [ROWS, H, COLS], BF16) for p in range(2)]
        qk_f = sb("qk_f", [P, GROUPS, COLS])
        qk_r = sb("qk_r", [P, GROUPS, COLS])
        qk_p = sb("qk_p", [P, 3, GROUPS, COLS], BF16)
        v_f = sb("v_f", [P, 3, D])
        v_r = sb("v_r", [P, 3, D])
        vp = sb("vp", [P, 3, H, HV], BF16)
        mx = sb("mx", [P, TB, 2, H])
        mparts = sb("mparts", [P, TB, 2, 2, H], BF16)
        mT = sb("mT", [4 * H, S], BF16)
        pf = [sb(f"pf{p}", [P, QUAD_COLS]) for p in range(3)]
        pl = [sb(f"pl{p}", [P, QUAD_COLS], F16) for p in range(2)]
        osum = [sb(f"osum{p}", [P, UNITS, HD]) for p in range(2)]
        rden = [sb(f"rden{p}", [P, UNITS]) for p in range(2)]
        onorm = sb("onorm", [P, UNITS, HD])
        att = sb("att", [P, TB, H, HD])
        attT = sb("attT", [P, KC, S])
        xb = sb("xb", [P, TB, D])
        y = sb("y", [P, TB, D])
        stats = sb("stats", [P, TB, 6])
        mv = sb("mv", [P, TB, 2])
        ve = sb("ve", [P, TB])
        rstd = sb("rstd", [P, TB])
        scaled = sb("scaled", [P, TB, D])
        n1 = sb("n1", [P, TB, D])
        nT = sb("nT", [P, KC, S])
        nb = sb("nb", [P, TB, D])
        hid = sb("hid", [P, FC, S])
        z = y
        h1 = sb("h1", [P, TB, D])
        hT = sb("hT", [P, KC, S])
        nm = sb("nm", [P, TB])
        nms = sb("nms", [P, TB])
        p2 = sb("p2", [P, TB, SE])
        den2 = sb("den2", [P, TB])
        rden2 = sb("rden2", [P, TB])
        p2T = sb("p2T", [SE, S])
        x2 = sb("x2", [P, TB, D])
        x2T = sb("x2T", [P, KC, S])
        x2b = n1
        r2T = sb("r2T", [P, KC, S])
        o_sb = sb("o_sb", [P, TB, D])

        scb = [bank(f"score_bank{n}") for n in range(SC_BANKS)]
        ob = [bank("o_bank0"), bank("o_bank1")]
        ga = bank("ga_bank")
        gc = [bank("gc_bank0"), bank("gc_bank1")]

        wqk_in = sem("wqk_in")
        wv_in = sem("wv_in")
        w_in = sem("w_in")
        wo_ready = sem("wo_ready")
        const_pool = sem("const_pool")
        const_dve = sem("const_dve")
        const_dma = sem("const_dma")
        mask_in = sem("mask_in")
        x_in = [sem("x_in0"), sem("x_in1")]
        tok_in = [sem("tok_in0"), sem("tok_in1")]
        stack_in = [sem("stack_in0"), sem("stack_in1")]
        max_in = [sem("max_in0"), sem("max_in1")]
        parts_out = sem("parts_out")
        out_done = [sem("out_done0"), sem("out_done1")]
        qk_ready = sem("qk_ready")
        qk_evac = sem("qk_evac")
        qk_hi, qk_rest, qk_mid, qk_low = (sem(n) for n in ("qk_hi", "qk_rest", "qk_mid", "qk_low"))
        v_ready = sem("v_ready")
        v_evac = sem("v_evac")
        v_hi, v_rest, v_mid, v_low = (sem(n) for n in ("v_hi", "v_rest", "v_mid", "v_low"))
        s_ready = sem("s_ready")
        s_done = sem("s_done")
        m_hi = sem("m_hi")
        m_low = sem("m_low")
        mt_ready = sem("mt_ready")
        mt_evac = sem("mt_evac")
        t_ready = sem("t_ready")
        t_done = sem("t_done")
        causal_done = sem("causal_done")
        pl_self = sem("pl_self")
        pl_cross = sem("pl_cross")
        pv_ready = sem("pv_ready")
        rden_ready = sem("rden_ready")
        pv_evac = sem("pv_evac")
        onorm_ready = sem("onorm_ready")
        att_ready = sem("att_ready")
        gc0_ready = sem("gc0_ready")
        gc0_evac = sem("gc0_evac")
        up_ready = sem("up_ready")
        gc1_ready = sem("gc1_ready")
        gc1_evac = sem("gc1_evac")
        xb_ready = sem("xb_ready")
        stat_ready = sem("stat_ready")
        mv_ready = sem("mv_ready")
        ve_ready = sem("ve_ready")
        rstd_ready = sem("rstd_ready")
        scaled_ready = sem("scaled_ready")
        n_ready = sem("n_ready")
        h_ready = sem("h_ready")
        nb_ready = sem("nb_ready")
        gelu_done = sem("gelu_done")
        relu_half = sem("relu_half")
        mask_float = sem("mask_float")
        nm_raw = sem("nm_raw")
        nm_ready = sem("nm_ready")
        p2_ready = sem("p2_ready")
        rden2_ready = sem("rden2_ready")
        x2_ready = sem("x2_ready")
        x2b_ready = sem("x2b_ready")
        o_ready = sem("o_ready")

        block = ctx.enter_context(nc.Block())

        def run(eng, body, before):
            def python_body(i):
                if i in before:
                    before[i]()
                body(i, lambda n: Seq(n, n // 2, n % 2) if 0 <= n < B else None)

            for i in range(-2, 2):
                python_body(i)
            with eng.Fori(0, (B - 4) // 2) as j:
                for u in range(2):
                    body(None, lambda k, u=u: Seq(2 * j + (2 + u + k), j + (2 + u + k) // 2, (u + k) % 2))
            for i in range(B - 2, B + 1):
                python_body(i)

        def high(t):
            return t.bitcast(BF16).rearrange("p (c two) -> p c two", two=2)[:, :, 1]

        def twice(t):
            return t[:, :].rearrange("p (o d) -> p o d", o=1).broadcast_to([P, TB, D])

        def score_bank(k):
            return scb[k % SC_BANKS]

        def seqs(i, at):
            return [at(k if i is None else i + k) for k in (-1, 0, 1, 2)]

        @block.sync
        def _(sp):
            def load_x(s):
                sp.dma_start(xTs[s.par][:, :, :], xT[s.n]).then_inc(x_in[s.par], 16)
                sp.dma_start(cTs[s.par][:, :, :], ctxT[s.n]).then_inc(x_in[s.par], 16)

            sp.dma_start(mask_i[:, :], mask[:, :]).then_inc(mask_in, 16)
            sp.dma_start(xTs[0][:, :, :], xT[0]).then_inc(x_in[0], 16)
            sp.dma_start(cTs[0][:, :, :], ctxT[0]).then_inc(x_in[0], 16)
            sp.dma_start(wqk[:, :, :, :, :], w_qk).then_inc(wqk_in, 16)
            sp.dma_start(bqk[:, :, :], b_qk).then_inc(wqk_in, 16)
            load_x(Seq(1, 0, 1))
            sp.dma_start(wv[:, :, :], w_v).then_inc(wv_in, 16)
            sp.dma_start(bvs[:, :], b_v.partition_broadcast(P)).then_inc(wv_in, 16)
            sp.dma_start(bos[:, :], b_o.partition_broadcast(P)).then_inc(wv_in, 16)
            sp.wait_ge(const_dve, N_CONST_DVE)
            for p in range(2):
                for row, col, width in ((ROW_SELF, COL_K, S), (ROW_CROSS, COL_C, SE)):
                    sp.dma_start(stack[p][row:row + 2, :, col:col + width],
                                 ones[:, 0:width].rearrange("p (o c) -> p o c", o=1)
                                 .broadcast_to([2, H, width])).then_inc(const_dma, 16)
            sp.dma_start(mask_dram[:, :, :], mask_p[:, :, :]).then_inc(const_dma, 16)
            sp.wait_ge(const_dma, 16 * N_CONST_DMA)

            def other_weights():
                loads = [(wo[:, :, :], w_o), (wfc[:, :, :], w_fc), (bfc[:, :], b_fc), (wm[:, :, :], w_m),
                         (w1s[:, :, :], w1T), (b1s[:, :], b1), (w2s[:, :, :], w2T)]
                loads += [(t[:, :], v.partition_broadcast(P)) for t, v in ((g1s, g1), (be1s, be1), (g2s, g2), (be2s, be2),
                                                                           (bms, b_m), (b2s, b2))]
                for dst, src in loads:
                    sp.dma_start(dst, src).then_inc(w_in, 16)
                assert len(loads) == N_LOADS

            def stack_reads(s):
                wait(sp, t_ready, T_BANKS * (s.n - 1))
                st = stack[s.par]
                sp.dma_start(st[ROW_MASK:ROW_MASK + 2, :, COL_C:COLS],
                             mask_dram[s.n].rearrange("r (o c) -> r o c", o=1).broadcast_to([2, H, SE])
                             ).then_inc(stack_in[s.par], 16)
                sp.wait_ge(parts_out, 16 * (s.n + 1))
                src = parts_dram.rearrange("a (d h) g c -> (a d) (h g) c", d=HD)
                done = 0
                for rows, parts in ((0, 3), (3, 2), (5, 1)):
                    sp.dma_start(st[rows * HD:(rows + parts) * HD, :, COL_Q:COL_Q + S],
                                 src[0:parts * HD, :, COL_Q:COL_Q + S]).then_inc(stack_in[s.par], 16)
                    done += 1
                for slot, part in enumerate(K_PARTS):
                    sp.dma_start(st[slot * HD:(slot + 1) * HD, :, COL_K:COLS],
                                 src[part * HD:(part + 1) * HD, :, COL_K:COLS]).then_inc(stack_in[s.par], 16)
                    done += 1
                assert done == MAIN_READS

            def body(i, at):
                c, a, b, q = seqs(i, at)
                if q and (i is None or q.n >= 2):
                    sp.wait_ge(v_ready, 2 * (q.n - 1))
                    load_x(q)
                if a:
                    wait(sp, gc1_ready, 5 * (a.n - 1))
                    wait(sp, xb_ready, a.n - 1)
                    sp.dma_start(xt[a.par][:, :, :], x[a.n]).then_inc(tok_in[a.par], 16)
                    sp.dma_start(ct[a.par][:, :], ctx_t[a.n]).then_inc(tok_in[a.par], 16)
                    sp.dma_start(cTt[a.par][:, :, :], ctxT[a.n]).then_inc(tok_in[a.par], 16)
                if a:
                    sp.wait_ge(mt_evac, a.n + 1)
                    for r in range(4):
                        sp.dma_start(stack[a.par][ROW_SELF + r:ROW_SELF + r + 1, :, COL_Q:COL_Q + S],
                                     mT[r * H:(r + 1) * H, :]).then_inc(max_in[a.par], 16)
                if b:
                    sp.wait_ge(qk_hi, b.n + 1)
                    sp.wait_ge(qk_mid, b.n + 1)
                    sp.wait_ge(qk_low, b.n + 1)
                    if a:
                        sp.wait_ge(stack_in[a.par], 16 * (MAIN_READS + 1) * (a.half + 1))
                    sp.dma_start(parts_dram.rearrange("a p g c -> p a g c"), qk_p[:, :, :, :]).then_inc(parts_out, 16)
                if b:
                    stack_reads(b)
                if c:
                    sp.wait_ge(o_ready, c.n + 1)
                    sp.dma_start(out[c.n], o_sb[:, :, :]).then_inc(out_done[c.par], 16)

            run(sp, body, {0: other_weights})
            for p in range(2):
                sp.wait_ge(out_done[p], 16 * (B // 2))

        @block.tensor
        def _(pe):
            pe.wait_ge(wqk_in, 32)

            def before_v():
                pe.wait_ge(wv_in, 48)

            def before_scores():
                pe.wait_ge(const_pool, N_CONST_POOL)
                pe.wait_ge(const_dve, N_CONST_DVE)
                pe.wait_ge(const_dma, 16 * N_CONST_DMA)

            def before_tail():
                pe.wait_ge(w_in, 16 * N_LOADS)
                pe.wait_ge(wo_ready, 1)

            def numerators(s, q, banks):
                st = stack[s.par]
                if q == 0 and 0 in banks:
                    pe.wait_ge(max_in[s.par], 64 * (s.half + 1))
                for n in banks:
                    m = 5 * q + n
                    t = score_bank(S_BANKS + m)
                    if m < SC_BANKS:
                        last = max(k for k in range(S_BANKS) if (S_BANKS + m - k) % SC_BANKS == 0)
                        pe.wait_ge(s_done, S_BANKS * s.n + last + 1)
                    else:
                        pe.wait_ge(t_done, T_BANKS * s.n + m - SC_BANKS + 1)
                    heads = {0: (0, 1), 1: (2, 3), 2: (0, 1, 2, 3), 3: (0, 1), 4: (2, 3)}[n]
                    for e, h4 in enumerate(heads):
                        h = QH * q + h4
                        first, last = e == 0, e == len(heads) - 1
                        if n < 2:
                            mm = nc.tensor.matmul(t[:, e * S:(e + 1) * S], st[0:ROWS, h, COL_K:COL_K + P],
                                                  st[0:ROWS, h, COL_Q:COL_Q + S], start=first, stop=last,
                                                  skip_group_check=True)
                        elif n == 2:
                            mm = nc.tensor.matmul(t[:, e * P:(e + 1) * P], st[0:ROWS, h, COL_K + P:COL_K + S],
                                                  st[0:ROWS, h, COL_Q + P:COL_Q + S], start=first, stop=last,
                                                  skip_group_check=True)
                        else:
                            mm = nc.tensor.matmul(t[0:SE, e * S:(e + 1) * S], st[0:ROWS, h, COL_C:COLS],
                                                  st[0:ROWS, h, COL_Q:COL_Q + S], start=first, stop=last,
                                                  skip_group_check=True)
                    mm.then_inc(t_ready, 1)

            def products(s, q, qb):
                qn = 4 * s.n + q
                if qb == 0:
                    pe.wait_ge(pl_self, qn + 1)
                    pe.wait_ge(pl_cross, qn + 1)
                if q == 0 and qb == 0:
                    pe.wait_ge(v_hi, s.n + 1)
                    pe.wait_ge(v_mid, s.n + 1)
                    pe.wait_ge(v_low, s.n + 1)
                    pe.wait_ge(mt_evac, s.n + 1)
                else:
                    wait(pe, pv_evac, 2 * (qn - 1) + qb + 1)
                first = True
                for h4 in range(QH):
                    for e in range(2):
                        u = 2 * h4 + e
                        if e == 0:
                            blocks = [(0, P, SELF0 + h4 * S + qb * P)]
                            if qb == 1:
                                blocks.append((1, P, SELF1 + h4 * P))
                        else:
                            blocks = [(2, SE, CROSS + h4 * S + qb * P)]
                        for blk, rows, col in blocks:
                            for w in (high(pf[q % 3][0:rows, col:col + P]), pl[q % 2][0:rows, col:col + P]):
                                mm = nc.tensor.matmul(ob[qb][:, u * HV:(u + 1) * HV], w,
                                                      vp[0:rows, blk, QH * q + h4, :],
                                                      start=first, stop=False, skip_group_check=True)
                                first = False
                mm.then_inc(pv_ready, 1)

            def row_scores(s, banks):
                st = stack[s.par]
                R = ROW_SELF
                for m in banks:
                    if m == 0:
                        pe.wait_ge(stack_in[s.par], 16 * (MAIN_READS + 1) * (s.half + 1))
                    t = score_bank(m)
                    if m < SC_BANKS:
                        last = max(k for k in range(T_BANKS) if (S_BANKS + k) % SC_BANKS == m)
                        wait(pe, t_done, T_BANKS * (s.n - 1) + last + 1)
                    else:
                        pe.wait_ge(s_done, S_BANKS * s.n + m - SC_BANKS + 1)
                    if m < 8:
                        o = t[:, :].rearrange("p (a c) -> p a c", a=2)
                        nc.tensor.matmul(o[:, :, P:S], identb[:, :], causal[:, 0:2, :], start=True, stop=False,
                                         skip_group_check=True)
                        for a in range(2):
                            h = 2 * m + a
                            mm = nc.tensor.matmul(o[:, a, :], st[0:R, h, COL_Q + P:COL_Q + S],
                                                  st[0:R, h, COL_K:COL_K + S], start=False, stop=a == 1,
                                                  skip_group_check=True)
                    elif m < 12:
                        o = t[:, :].rearrange("p (a c) -> p a c", a=4)
                        nc.tensor.matmul(o, identb[:, :], causal[:, :, :], start=True, stop=False,
                                         skip_group_check=True)
                        for a in range(4):
                            h = 4 * (m - 8) + a
                            mm = nc.tensor.matmul(o[:, a, :], st[0:R, h, COL_Q:COL_Q + P],
                                                  st[0:R, h, COL_K:COL_K + P], start=False, stop=a == 3,
                                                  skip_group_check=True)
                    else:
                        qb, run_ = divmod(m - 12, 3)
                        heads = range(CROSS_RUN * run_, min(CROSS_RUN * run_ + CROSS_RUN, H))
                        for a, h in enumerate(heads):
                            mm = nc.tensor.matmul(t[:, a * SE:(a + 1) * SE], st[0:R, h, COL_Q + qb * P:COL_Q + (qb + 1) * P],
                                                  st[0:R, h, COL_C:COLS], start=a == 0, stop=a == len(heads) - 1,
                                                  skip_group_check=True)
                    mm.then_inc(s_ready, 1)

            def max_transposes(s):
                pe.wait_ge(m_low, s.n + 1)
                wait(pe, pv_evac, 8 * s.n)
                for t in range(TB):
                    mm = nc.tensor.matmul(ob[0][0:4 * H, t * P:(t + 1) * P],
                                          mparts[:, t, :, :, :].rearrange("p a b h -> p (a b h)"), identb[:, :],
                                          start=t == 0, stop=True, skip_group_check=True)
                mm.then_inc(mt_ready, 1)

            def values(s, t):
                if t == 0:
                    pe.wait_ge(x_in[s.par], 32 * (s.half + 1))
                    pe.wait_ge(qk_evac, min(6 * s.n + 8, 6 * B) if isinstance(s.n, int) else 6 * s.n + 8)
                    wait(pe, gelu_done, 8 * (s.n - 1))
                if t == 2:
                    pe.wait_ge(v_evac, 2 * s.n + 1)
                for k in range(KC):
                    if t < 2:
                        mm = nc.tensor.matmul(ga[:, t * D:(t + 1) * D], xTs[s.par][:, k, t * P:(t + 1) * P], wv[:, k, :],
                                              start=t == 0 and k == 0, stop=k == KC - 1, skip_group_check=True)
                    else:
                        mm = nc.tensor.matmul(ga[0:SE, 0:D], cTs[s.par][:, k, :], wv[:, k, :], start=k == 0,
                                              stop=k == KC - 1)
                if t > 0:
                    mm.then_inc(v_ready, 1)

            def queries(s, step, g):
                if g == 0:
                    if step == 0:
                        pe.wait_ge(x_in[s.par], 32 * (s.half + 1))
                        wait(pe, qk_evac, 6 * s.n)
                        wait(pe, gelu_done, 8 * (s.n - 2))
                    else:
                        pe.wait_ge(qk_evac, 6 * s.n + 2 * step)
                        wait(pe, v_evac, 2 * s.n)
                which, src, width = ((1, xTs, S), (0, xTs, S), (1, cTs, SE))[step]
                for k in range(KC):
                    mm = nc.tensor.matmul(ga[:, g * width:(g + 1) * width], wqk[:, k, which, g, :], src[s.par][:, k, :],
                                          start=g == 0 and k == 0, stop=k == KC - 1, skip_group_check=True)
                if g == GROUPS - 1:
                    mm.then_inc(qk_ready, 1)

            def into_gc1(s, use):
                wait(pe, gc1_evac, 5 * s.n + use)

            def transposes(src, dst):
                for k in range(KC):
                    for t in range(TB):
                        mm = nc.tensor.transpose(dst[:, k * S + t * P:k * S + (t + 1) * P],
                                                 src[:, t, k * P:(k + 1) * P], ident[:, :])
                return mm

            def by_token(dst, lhs, rhs, t):
                for k in range(KC):
                    mm = nc.tensor.matmul(dst[:, t * D:(t + 1) * D], lhs[:, k, t * P:(t + 1) * P], rhs[:, k, :],
                                          start=t == 0 and k == 0, stop=k == KC - 1, skip_group_check=True)
                return mm

            def up(s, j, e):
                dst = (gc[0], ga)[j % 2]
                if e == 0:
                    if j == 0:
                        pe.wait_ge(gc0_evac, 3 * s.n + 2)
                    elif j == 1:
                        pe.wait_ge(qk_evac, 6 * (min(s.n + 3, B) if isinstance(s.n, int) else s.n + 3))
                    else:
                        pe.wait_ge(gelu_done, 8 * s.n + 2 * (j - 2) + 2)
                f = 2 * j + e
                for k in range(KC):
                    mm = nc.tensor.matmul(dst[:, e * S:(e + 1) * S], wfc[:, k, f * P:(f + 1) * P], nT[:, k, :],
                                          start=e == 0 and k == 0, stop=k == KC - 1, skip_group_check=True)
                if e == 1:
                    mm.then_inc(up_ready, 1)

            def down(s, j, e):
                f = 2 * j + e
                if e == 0:
                    pe.wait_ge(gelu_done, 8 * s.n + 2 * j + 2)
                    if j == 0:
                        into_gc1(s, 1)
                for t in range(TB):
                    mm = nc.tensor.matmul(gc[1][:, t * D:(t + 1) * D], hid[:, f, t * P:(t + 1) * P], wm[:, f, :],
                                          start=f == 0 and t == 0, stop=f == FC - 1, skip_group_check=True)
                if f == FC - 1:
                    mm.then_inc(gc1_ready, 1)

            def scores2(s, t):
                if t == 0:
                    pe.wait_ge(gc0_evac, 3 * s.n + 3)
                    pe.wait_ge(tok_in[s.par], 48 * (s.half + 1))
                for k in range(KC):
                    mm = nc.tensor.matmul(gc[0][:, t * SE:(t + 1) * SE], hT[:, k, t * P:(t + 1) * P], cTt[s.par][:, k, :],
                                          start=t == 0 and k == 0, stop=k == KC - 1, skip_group_check=True)
                if t == TB - 1:
                    mm.then_inc(gc0_ready, 1)

            def relu_in(s, f):
                if f == 0:
                    pe.wait_ge(gc1_evac, 5 * s.n + 4)
                for k in range(KC):
                    mm = nc.tensor.matmul(gc[0][:, f * S:(f + 1) * S], w1s[:, k, f * P:(f + 1) * P], x2T[:, k, :],
                                          start=f == 0 and k == 0, stop=k == KC - 1, skip_group_check=True)
                if f == KC - 1:
                    mm.then_inc(gc0_ready, 1)

            def att_transposes(s):
                pe.wait_ge(att_ready, 4 * s.n + 4)
                wait(pe, relu_half, 2 * s.n)
                transposes(att[:, :, :, :].rearrange("p t h d -> p t (h d)"), gc[0]).then_inc(gc0_ready, 1)

            def output_projection(s):
                pe.wait_ge(gc0_evac, 3 * s.n + 1)
                into_gc1(s, 0)
                by_token(gc[1], attT, wo, 0)
                by_token(gc[1], attT, wo, 1).then_inc(gc1_ready, 1)

            def n_transposes(s):
                pe.wait_ge(n_ready, 2 * s.n + 2)
                transposes(n1, gc[0]).then_inc(gc0_ready, 1)

            def h_transposes(s):
                pe.wait_ge(h_ready, 2 * s.n + 2)
                pe.wait_ge(gelu_done, 8 * s.n + 6)
                transposes(h1, gc[0]).then_inc(gc0_ready, 1)

            def numerator2_transposes(s):
                pe.wait_ge(p2_ready, 2 * s.n + 2)
                into_gc1(s, 2)
                for t in range(TB):
                    mm = nc.tensor.transpose(gc[1][0:SE, t * P:(t + 1) * P], p2[:, t, :], ident[:, :])
                mm.then_inc(gc1_ready, 1)

            def products2(s):
                pe.wait_ge(gc1_evac, 5 * s.n + 3)
                for t in range(TB):
                    mm = nc.tensor.matmul(gc[0][:, t * D:(t + 1) * D], p2T[:, t * P:(t + 1) * P], ct[s.par][:, :],
                                          start=t == 0, stop=True, skip_group_check=True)
                mm.then_inc(gc0_ready, 1)

            def x2_transposes(s):
                pe.wait_ge(x2_ready, 2 * s.n + 2)
                into_gc1(s, 3)
                transposes(x2, gc[1]).then_inc(gc1_ready, 1)

            def relu_out(s, t):
                if t == 0:
                    pe.wait_ge(relu_half, 2 * s.n + 2)
                    into_gc1(s, 4)
                mm = by_token(gc[1], r2T, w2s, t)
                if t == TB - 1:
                    mm.then_inc(gc1_ready, 1)

            def body(i, at):
                c, a, b, q = seqs(i, at)

                def do(s, step, *args):
                    if s:
                        step(s, *args)

                do(a, row_scores, (0, 1, 2))
                do(c, att_transposes)
                do(a, row_scores, (3, 4))
                do(c, output_projection)
                do(b, queries, 1, 0)
                do(b, queries, 1, 1)
                do(a, row_scores, (5, 6))
                do(b, queries, 2, 0)
                do(b, queries, 2, 1)
                do(a, row_scores, (7,))
                do(c, n_transposes)
                do(a, row_scores, (8, 9))
                do(c, up, 0, 0)
                do(a, row_scores, (10, 11))
                do(c, up, 0, 1)
                do(a, row_scores, (12,))
                do(c, up, 1, 0)
                do(a, row_scores, (13, 14))
                do(c, up, 1, 1)
                do(a, row_scores, (15,))
                do(c, down, 0, 0)
                do(a, row_scores, (16,))
                do(c, down, 0, 1)
                do(a, row_scores, (17,))
                do(c, up, 2, 0)
                do(c, up, 2, 1)
                do(a, max_transposes)
                do(c, down, 1, 0)
                do(c, down, 1, 1)
                do(c, up, 3, 0)
                do(c, up, 3, 1)
                do(c, down, 2, 0)
                do(c, down, 2, 1)
                do(a, numerators, 0, (0,))
                do(c, down, 3, 0)
                do(a, numerators, 0, (1, 2))
                do(c, down, 3, 1)
                do(a, numerators, 0, (3, 4))
                do(q, queries, 0, 0)
                do(a, numerators, 1, (0,))
                do(q, queries, 0, 1)
                do(a, numerators, 1, (1, 2, 3))
                do(b, values, 0)
                do(b, values, 1)
                do(c, h_transposes)
                do(a, numerators, 1, (4,))
                do(a, numerators, 2, (0,))
                do(a, products, 0, 0)
                do(c, scores2, 0)
                do(c, scores2, 1)
                do(a, numerators, 2, (1,))
                do(a, products, 0, 1)
                do(a, numerators, 2, (2, 3))
                do(a, products, 1, 0)
                do(c, numerator2_transposes)
                do(a, numerators, 2, (4,))
                do(a, products, 1, 1)
                do(a, numerators, 3, (0,))
                do(c, products2)
                do(a, numerators, 3, (1, 2, 3))
                do(b, values, 2)
                do(c, x2_transposes)
                do(a, numerators, 3, (4,))
                do(a, products, 2, 0)
                do(c, relu_in, 0)
                do(c, relu_in, 1)
                do(a, products, 2, 1)
                do(a, products, 3, 0)
                do(c, relu_out, 0)
                do(a, products, 3, 1)
                do(c, relu_out, 1)

            run(pe, body, {-1: before_v, 0: before_scores, 1: before_tail})

        @block.scalar
        def _(act):
            act.wait_ge(wqk_in, 32)

            def before_tail():
                act.wait_ge(w_in, 16 * N_LOADS)

            def exps(s, q, banks):
                if 0 in banks:
                    wait(act, pv_ready, 8 * s.n + (2 if q == 3 else 0))
                dst = pf[q % 3]
                places = ((P, SELF0), (P, SELF0 + 512), (P, SELF1), (SE, CROSS), (SE, CROSS + 512))
                for n in banks:
                    rows, col = places[n]
                    m = 5 * q + n
                    act.wait_ge(t_ready, T_BANKS * s.n + m + 1)
                    nc.scalar.activation(dst[0:rows, col:col + 512], score_bank(S_BANKS + m)[0:rows, :], ACT.Exp,
                                         scale=HD ** -0.5).then_inc(t_done, 1)

            def queries_out(s, step):
                if step == 0:
                    wait(act, qk_hi, s.n)
                    wait(act, qk_rest, s.n)
                which, col, width = ((1, COL_K, S), (0, COL_Q, S), (1, COL_C, SE))[step]
                act.wait_ge(qk_ready, 3 * s.n + step + 1)
                for g in range(GROUPS):
                    nc.scalar.activation(qk_f[:, g, col:col + width], ga[:, g * width:(g + 1) * width], ACT.Identity,
                                         bias=bqk[:, which, g:g + 1]).then_inc(qk_evac, 1)

            def gelu(s, j):
                act.wait_ge(up_ready, 4 * s.n + j + 1)
                if j == 0:
                    wait(act, gc1_ready, 5 * (s.n - 1) + 2)
                for e in range(2):
                    f = 2 * j + e
                    nc.scalar.activation(hid[:, f, :], (gc[0], ga)[j % 2][:, e * S:(e + 1) * S], ACT.Gelu_apprx_tanh,
                                         bias=bfc[:, f:f + 1]).then_inc(gelu_done, 1)

            def from_gc0(s, use, dst, src):
                act.wait_ge(gc0_ready, 6 * s.n + use)
                nc.scalar.activation(dst, src, ACT.Copy).then_inc(gc0_evac, 1)

            def from_gc1(s, use, dst, src):
                act.wait_ge(gc1_ready, 5 * s.n + use)
                nc.scalar.activation(dst, src, ACT.Copy).then_inc(gc1_evac, 1)

            def flat(t):
                return t[:, :, :].rearrange("p k s -> p (k s)")

            def body(i, at):
                c, a, b, q = seqs(i, at)
                if c:
                    from_gc0(c, 1, flat(attT), gc[0][:, :])
                if b:
                    queries_out(b, 1)
                    queries_out(b, 2)
                if c:
                    from_gc0(c, 2, flat(nT), gc[0][:, :])
                    gelu(c, 0)
                    gelu(c, 1)
                    gelu(c, 2)
                if a:
                    act.wait_ge(mt_ready, a.n + 1)
                    wait(act, max_in[1 - a.par], 64 * (a.half + a.par))
                    nc.scalar.activation(mT[:, :], ob[0][0:4 * H, 0:S], ACT.Copy).then_inc(mt_evac, 1)
                if c:
                    gelu(c, 3)
                if a:
                    exps(a, 0, range(0, 5))
                    exps(a, 1, (0,))
                if q:
                    queries_out(q, 0)
                if a:
                    exps(a, 1, (1, 2, 3))
                if c:
                    from_gc0(c, 3, flat(hT), gc[0][:, :])
                if a:
                    exps(a, 1, (4,))
                    exps(a, 2, (0, 1))
                if c:
                    act.wait_ge(nm_ready, c.n + 1)
                    wait(act, gc1_ready, 5 * (c.n - 1) + 3)
                    wait(act, rden2_ready, c.n)
                    for t in range(TB):
                        nc.scalar.activation(p2[:, t, :], gc[0][:, t * SE:(t + 1) * SE], ACT.Exp, scale=D ** -0.5,
                                             bias=nms[:, t:t + 1], accum_out=den2[:, t:t + 1]).then_inc(p2_ready, 1)
                if a:
                    exps(a, 2, (2, 3))
                if c:
                    from_gc1(c, 3, p2T[:, :], gc[1][0:SE, 0:S])
                if a:
                    exps(a, 2, (4,))
                    exps(a, 3, (0, 1, 2, 3))
                if c:
                    from_gc1(c, 4, flat(x2T), gc[1][:, :])
                if a:
                    exps(a, 3, (4,))
                if c:
                    act.wait_ge(gc0_ready, 6 * c.n + 6)
                    for f in range(KC):
                        nc.scalar.activation(r2T[:, f, :], gc[0][:, f * S:(f + 1) * S], ACT.Relu,
                                             bias=b1s[:, f:f + 1]).then_inc(relu_half, 1)

            run(act, body, {1: before_tail})

        @block.vector
        def _(dve):
            v = nc.vector
            v.memset(ones[:, :], 1.0).then_inc(const_dve, 1)
            for p in range(2):
                v.memset(stack[p][ROW_MASK:ROWS, :, COL_Q:COL_Q + S], 1.0).then_inc(const_dve, 1)
                v.memset(stack[p][ROW_MASK:ROWS, :, COL_K:COLS], 0.0).then_inc(const_dve, 1)
            dve.wait_ge(mask_in, 16)
            v.tensor_copy(mask_f[:, :], mask_i[:, :]).then_inc(mask_float, 1)
            dve.wait_ge(mask_float, 1)
            v.tensor_scalar(mask_p[:, 0, :], mask_f[:, :], -99840.0 * HD ** 0.5, None, ALU.mult)
            v.tensor_scalar(mask_p[:, 1, :], mask_f[:, :], (NEG + 99840.0) * HD ** 0.5, None,
                            ALU.mult).then_inc(const_dve, 1)
            v.memset(half_pow[:, :], -0.5).then_inc(const_dve, 1)
            v.memset(vp[:, :, :, V_PARTS * HD:HV], 1.0).then_inc(const_dve, 1)
            v.memset(v_f[:, 2, :], 0.0).then_inc(const_dve, 1)
            dve.wait_ge(const_dve, N_CONST_DVE)

            def before_v():
                dve.wait_ge(wv_in, 48)

            def before_tail():
                dve.wait_ge(w_in, 16 * N_LOADS)

            def heads(t, blk=slice(0, 3)):
                return t[:, blk, :].rearrange("p b (h d) -> p (b h) d", d=HD)

            def part(k):
                return vp[:, :, :, k * HD:(k + 1) * HD].rearrange("p b h d -> p (b h) d")

            def low_self(s, q):
                qn = 4 * s.n + q
                wait(dve, pv_ready, 2 * (qn - 1))
                dve.wait_ge(causal_done, 2 * qn + 2)
                v.tensor_tensor(pl[q % 2][:, 0:CROSS], pf[q % 3][:, 0:CROSS], high(pf[q % 3][:, 0:CROSS]),
                                ALU.subtract).then_inc(pl_self, 1)

            def add_parts(s, q, qb):
                n = 2 * (4 * s.n + q) + qb
                units = slice(qb * HALF_UNITS, (qb + 1) * HALF_UNITS)
                o = ob[qb][:, 0:HALF_UNITS * HV].rearrange("p (u c) -> p u c", c=HV)
                dve.wait_ge(pv_ready, n + 1)
                if qb == 0:
                    wait(dve, onorm_ready, 4 * s.n + q - 1)
                v.reciprocal(rden[q % 2][:, units], o[:, :, V_PARTS * HD]).then_inc(rden_ready, 1)
                v.tensor_reduce(osum[q % 2][:, units, :], o[:, :, 0:V_PARTS * HD].rearrange("p u (k d) -> p u d k", d=HD),
                                AX_X, ALU.add).then_inc(pv_evac, 1)

            def norm(s, q):
                qn = 4 * s.n + q
                dve.wait_ge(rden_ready, 2 * qn + 2)
                dve.wait_ge(pv_evac, 2 * qn + 2)
                wait(dve, att_ready, qn)
                r = rden[q % 2][:, :]
                rb = bass.AP(r.tensor, r.offset, [[UNITS, P], [1, UNITS], [0, HD]])
                v.tensor_tensor(onorm[:, :, :], osum[q % 2][:, :, :], rb, ALU.mult).then_inc(onorm_ready, 1)
                dve.wait_ge(onorm_ready, qn + 1)
                if q == 0:
                    wait(dve, gc0_ready, 6 * (s.n - 1) + 1)
                on = onorm[:, :, :].rearrange("p (t h a) d -> p a t h d", t=TB, a=2)
                for t in range(TB):
                    ins = v.tensor_tensor(att[:, t, QH * q:QH * q + QH, :], on[:, 0, t], on[:, 1, t], ALU.add)
                ins.then_inc(att_ready, 1)

            def row_max(s, banks):
                for m in banks:
                    dve.wait_ge(s_ready, S_BANKS * s.n + m + 1)
                    if m == 0:
                        wait(dve, m_low, s.n)
                    t = score_bank(m)
                    if m < 8:
                        src, dst = t[:, :].rearrange("p (a c) -> p a c", a=2), mx[:, 1, 0, 2 * m:2 * m + 2]
                    elif m < 12:
                        src, dst = t[:, :].rearrange("p (a c) -> p a c", a=4), mx[:, 0, 0, 4 * (m - 8):4 * (m - 7)]
                    else:
                        qb, run_ = divmod(m - 12, 3)
                        h0, h1_ = CROSS_RUN * run_, min(CROSS_RUN * run_ + CROSS_RUN, H)
                        src = t[:, 0:(h1_ - h0) * SE].rearrange("p (a c) -> p a c", c=SE)
                        dst = mx[:, qb, 1, h0:h1_]
                    v.tensor_reduce(dst, src, AX_X, ALU.max, negate=True).then_inc(s_done, 1)

            def max_parts(s):
                dve.wait_ge(s_done, S_BANKS * (s.n + 1))
                wait(dve, mt_ready, s.n)
                for t in range(TB):
                    ins = v.tensor_copy(mparts[:, t, :, 0, :], mx[:, t, :, :])
                ins.then_inc(m_hi, 1)
                dve.wait_ge(m_hi, s.n + 1)
                for t in range(TB):
                    ins = v.tensor_tensor(mparts[:, t, :, 1, :], mx[:, t, :, :], mparts[:, t, :, 0, :], ALU.subtract)
                ins.then_inc(m_low, 1)

            def layer_stats(s, src, ln):
                for t in range(TB):
                    v.bn_stats(stats[:, t, :], src[:, t, :]).then_inc(stat_ready, 1)
                dve.wait_ge(stat_ready, 4 * s.n + 2 * ln + 2)
                v.memset(tick[:, 3:4], 0.0)
                for t in range(TB):
                    v.bn_aggr(mv[:, t, :], stats[:, t, :]).then_inc(mv_ready, 1)
                dve.wait_ge(mv_ready, 4 * s.n + 2 * ln + 2)
                v.tensor_scalar(ve[:, :], mv[:, :, 1], EPS, None, ALU.add).then_inc(ve_ready, 1)

            def layer_scale(s, src, gamma, ln):
                for t in range(TB):
                    v.scalar_tensor_tensor(scaled[:, t, :], src[:, t, :], mv[:, t, 0:1], gamma[:, :],
                                           ALU.subtract, ALU.mult).then_inc(scaled_ready, 1)

            def layer_out(s, dst, beta, ln, done):
                dve.wait_ge(scaled_ready, 4 * s.n + 2 * ln + 2)
                dve.wait_ge(rstd_ready, 2 * s.n + ln + 1)
                for t in range(TB):
                    v.scalar_tensor_tensor(dst[:, t, :], scaled[:, t, :], rstd[:, t:t + 1], beta[:, :],
                                           ALU.mult, ALU.add).then_inc(done, 1)

            def both(t):
                return t[:, :, :].rearrange("p t d -> p (t d)")

            def body(i, at):
                c, a, b, q = seqs(i, at)
                if a:
                    row_max(a, range(2, 5))
                if c:
                    dve.wait_ge(gc1_ready, 5 * c.n + 1)
                    dve.wait_ge(xb_ready, c.n + 1)
                    v.tensor_tensor(both(y), gc[1][:, :], both(xb), ALU.add).then_inc(gc1_evac, 1)
                    dve.wait_ge(gc1_evac, 5 * c.n + 1)
                    layer_stats(c, y, 0)
                    dve.wait_ge(mv_ready, 4 * c.n + 2)
                    layer_scale(c, y, g1s, 0)
                    layer_out(c, n1, be1s, 0, n_ready)
                if a:
                    row_max(a, range(5, 10))
                    dve.wait_ge(v_evac, 2 * a.n + 2)
                    wait(dve, pv_ready, 8 * a.n)
                    v.tensor_copy(part(0), heads(v_f)).then_inc(v_hi, 1)
                    row_max(a, range(10, S_BANKS))
                    max_parts(a)
                if b:
                    dve.wait_ge(qk_evac, 6 * (b.n + 1))
                    wait(dve, parts_out, 16 * b.n)
                    v.tensor_copy(qk_p[:, 0, :, :], qk_f[:, :, :]).then_inc(qk_hi, 1)
                if a:
                    dve.wait_ge(v_rest, a.n + 1)
                    v.tensor_copy(part(1), heads(v_r)).then_inc(v_mid, 1)
                if b:
                    dve.wait_ge(qk_rest, b.n + 1)
                    v.tensor_copy(qk_p[:, 1, :, :], qk_r[:, :, :]).then_inc(qk_mid, 1)
                if c:
                    dve.wait_ge(gc1_ready, 5 * c.n + 2)
                    dve.wait_ge(nb_ready, c.n + 1)
                    v.tensor_tensor(both(z), gc[1][:, :], both(nb), ALU.add).then_inc(gc1_evac, 1)
                    dve.wait_ge(gc1_evac, 5 * c.n + 2)
                    layer_stats(c, z, 1)
                    dve.wait_ge(mv_ready, 4 * c.n + 4)
                    layer_scale(c, z, g2s, 1)
                    layer_out(c, h1, be2s, 1, h_ready)
                if a:
                    low_self(a, 0)
                if b:
                    dve.wait_ge(v_ready, 2 * b.n + 1)
                    wait(dve, v_rest, b.n)
                    wait(dve, v_hi, b.n)
                    v.tensor_tensor(v_f[:, 0:2, :], ga[:, :].rearrange("p (t d) -> p t d", t=TB), twice(bvs),
                                    ALU.add).then_inc(v_evac, 1)
                if a:
                    low_self(a, 1)
                if c:
                    dve.wait_ge(gc0_ready, 6 * c.n + 4)
                    v.tensor_reduce(nm[:, :], gc[0][:, 0:TB * SE].rearrange("p (t c) -> p t c", t=TB), AX_X, ALU.max,
                                    negate=True).then_inc(nm_raw, 1)
                    dve.wait_ge(nm_raw, c.n + 1)
                    v.tensor_scalar(nms[:, :], nm[:, :], D ** -0.5, None, ALU.mult).then_inc(nm_ready, 1)
                if a:
                    add_parts(a, 0, 0)
                    add_parts(a, 0, 1)
                    norm(a, 0)
                    add_parts(a, 1, 0)
                    add_parts(a, 1, 1)
                if c:
                    dve.wait_ge(p2_ready, 2 * c.n + 2)
                    v.reciprocal(rden2[:, :], den2[:, :]).then_inc(rden2_ready, 1)
                    dve.wait_ge(rden2_ready, c.n + 1)
                    dve.wait_ge(gc0_ready, 6 * c.n + 5)
                    for t in range(TB):
                        v.scalar_tensor_tensor(x2[:, t, :], gc[0][:, t * D:(t + 1) * D], rden2[:, t:t + 1], h1[:, t, :],
                                               ALU.mult, ALU.add).then_inc(x2_ready, 1)
                if a:
                    low_self(a, 2)
                if b:
                    dve.wait_ge(v_ready, 2 * b.n + 2)
                    v.tensor_tensor(v_f[0:SE, 2, :], ga[0:SE, 0:D], bvs[0:SE, :], ALU.add).then_inc(v_evac, 1)
                if a:
                    low_self(a, 3)
                    add_parts(a, 2, 0)
                    add_parts(a, 2, 1)
                    add_parts(a, 3, 0)
                    norm(a, 2)
                    add_parts(a, 3, 1)
                    norm(a, 3)
                if b:
                    row_max(b, (0, 1))
                if c:
                    dve.wait_ge(gc1_ready, 5 * c.n + 5)
                    dve.wait_ge(x2b_ready, c.n + 1)
                    wait(dve, out_done[1 - c.par], 16 * (c.half + c.par))
                    v.tensor_tensor(both(o_sb), gc[1][:, :], both(x2b), ALU.add).then_inc(gc1_evac, 1)
                    dve.wait_ge(gc1_evac, 5 * c.n + 5)
                    v.memset(tick[:, 3:4], 0.0).then_inc(o_ready, 1)

            run(dve, body, {-1: before_v, 1: before_tail})

        @block.gpsimd
        def _(pool):
            g = nc.gpsimd
            g.memset(ident[:, :], 0.0).then_inc(const_pool, 1)
            g.memset(identb[:, :], 0.0).then_inc(const_pool, 1)
            g.memset(causal[:, :, :], -1e30).then_inc(const_pool, 1)
            g.memset(ptick[:, :], 0.0).then_inc(const_pool, 1)
            pool.wait_ge(const_pool, 4)
            for m in (ident, identb):
                g.affine_select(out=m[:, :], in_=m[:, :], compare_op=ALU.not_equal, fill=1.0, base=0,
                                pattern=[[-1, P]], channel_multiplier=1).then_inc(const_pool, 1)
            g.affine_select(out=causal[:, :, :], in_=causal[:, :, :], compare_op=ALU.is_gt, fill=0.0, base=0,
                            pattern=[[0, 4], [1, P]], channel_multiplier=-1).then_inc(const_pool, 1)
            pool.wait_ge(const_dve, N_CONST_DVE)
            pool.wait_ge(const_pool, N_CONST_POOL)

            def before_xb():
                pool.wait_ge(wv_in, 48)

            def before_tail():
                pool.wait_ge(w_in, 16 * N_LOADS)
                g.tensor_scalar(wo[:, :, :], wo[:, :, :], 0.5, None, ALU.mult).then_inc(wo_ready, 1)

            def carry(q):
                g.tensor_tensor(ptick[:, 2 + q:3 + q], ptick[:, 0:1], ptick[:, 1:2], ALU.add)

            def clear_masked(s, q):
                pool.wait_ge(t_done, T_BANKS * s.n + 5 * q + 3)
                carry(q)
                d0 = pf[q % 3][:, SELF0:SELF1].rearrange("p (h c) -> p h c", h=QH)[:, :, 0:P]
                d1 = pf[q % 3][:, SELF1:CROSS].rearrange("p (h c) -> p h c", h=QH)
                for d in (d0, d1):
                    g.affine_select(out=d, in_=d, compare_op=ALU.is_ge, fill=0.0, base=0,
                                    pattern=[[0, QH], [1, P]], channel_multiplier=-1).then_inc(causal_done, 1)

            def low_cross(s, q):
                qn = 4 * s.n + q
                wait(pool, pv_ready, 2 * (qn - 1))
                pool.wait_ge(t_done, T_BANKS * s.n + 5 * q + 5)
                g.tensor_tensor(pl[q % 2][0:SE, CROSS:QUAD_COLS], pf[q % 3][0:SE, CROSS:QUAD_COLS],
                                high(pf[q % 3][0:SE, CROSS:QUAD_COLS]), ALU.subtract).then_inc(pl_cross, 1)

            def norm(s, q):
                qn = 4 * s.n + q
                pool.wait_ge(rden_ready, 2 * qn + 2)
                pool.wait_ge(pv_evac, 2 * qn + 2)
                wait(pool, att_ready, qn)
                r = rden[q % 2][:, :]
                rb = bass.AP(r.tensor, r.offset, [[UNITS, P], [1, UNITS], [0, HD]])
                g.tensor_tensor(onorm[:, :, :], osum[q % 2][:, :, :], rb, ALU.mult).then_inc(onorm_ready, 1)
                pool.wait_ge(onorm_ready, qn + 1)
                if q == 0:
                    wait(pool, gc0_ready, 6 * (s.n - 1) + 1)
                on = onorm[:, :, :].rearrange("p (t h a) d -> p a t h d", t=TB, a=2)
                for t in range(TB):
                    ins = g.tensor_tensor(att[:, t, QH * q:QH * q + QH, :], on[:, 0, t], on[:, 1, t], ALU.add)
                ins.then_inc(att_ready, 1)

            def heads(t):
                return t[:, :, :].rearrange("p b (h d) -> p (b h) d", d=HD)

            def part(k):
                return vp[:, :, :, k * HD:(k + 1) * HD].rearrange("p b h d -> p (b h) d")

            def body(i, at):
                c, a, b, q = seqs(i, at)
                if c:
                    pool.wait_ge(ve_ready, 2 * c.n + 1)
                    g.tensor_tensor(rstd[:, :], ve[:, :], half_pow[:, :], ALU.pow).then_inc(rstd_ready, 1)
                if a:
                    pool.wait_ge(v_hi, a.n + 1)
                    wait(pool, v_mid, a.n)
                    g.tensor_tensor(heads(v_r), heads(v_f), part(0), ALU.subtract).then_inc(v_rest, 1)
                if b:
                    pool.wait_ge(qk_hi, b.n + 1)
                    g.tensor_tensor(qk_r[:, :, :], qk_f[:, :, :], qk_p[:, 0, :, :], ALU.subtract).then_inc(qk_rest, 1)
                if c:
                    pool.wait_ge(n_ready, 2 * c.n + 2)
                    wait(pool, gc1_evac, 5 * (c.n - 1) + 2)
                    g.tensor_tensor(nb[:, :, :], n1[:, :, :], twice(bms), ALU.add).then_inc(nb_ready, 1)
                if a:
                    pool.wait_ge(v_mid, a.n + 1)
                    g.tensor_tensor(part(2), heads(v_r), part(1), ALU.subtract).then_inc(v_low, 1)
                if b:
                    pool.wait_ge(qk_mid, b.n + 1)
                    g.tensor_tensor(qk_p[:, 2, :, :], qk_r[:, :, :], qk_p[:, 1, :, :], ALU.subtract).then_inc(qk_low, 1)
                if a:
                    clear_masked(a, 0)
                if c:
                    pool.wait_ge(ve_ready, 2 * c.n + 2)
                    g.tensor_tensor(rstd[:, :], ve[:, :], half_pow[:, :], ALU.pow).then_inc(rstd_ready, 1)
                if a:
                    low_cross(a, 0)
                    clear_masked(a, 1)
                    low_cross(a, 1)
                    clear_masked(a, 2)
                    low_cross(a, 2)
                    clear_masked(a, 3)
                    low_cross(a, 3)
                    norm(a, 1)
                if c:
                    pool.wait_ge(x2_ready, 2 * c.n + 2)
                    wait(pool, gc1_evac, 5 * c.n)
                    g.tensor_tensor(x2b[:, :, :], x2[:, :, :], twice(b2s), ALU.add).then_inc(x2b_ready, 1)
                if a:
                    pool.wait_ge(tok_in[a.par], 48 * (a.half + 1))
                    wait(pool, gc1_evac, 5 * (a.n - 1) + 1)
                    g.tensor_tensor(xb[:, :, :], xt[a.par][:, :, :], twice(bos), ALU.add).then_inc(xb_ready, 1)

            run(pool, body, {0: before_xb, 1: before_tail})


N_LOADS = 13
N_CONST_DMA = 2 * 2 + 1
N_CONST_POOL = 7
N_CONST_DVE = 9


def kernel(x, ctx_1024, mask_BxS2_ik0, L0_xattn_w_attn, L0_xattn_b_attn, L0_xattn_w_oproj, L0_xattn_b_oproj,
           L0_xattn_w_fc, L0_xattn_b_fc, L0_xattn_w_mproj, L0_xattn_b_mproj, L0_xattn_ln1_g, L0_xattn_ln1_b,
           L0_xattn_ln2_g, L0_xattn_ln2_b, L1_xattn_W1, L1_xattn_b1, L1_xattn_W2, L1_xattn_b2):
    import concourse.bacc as bacc
    from concourse.bass_utils import run_bass_kernel_spmd

    def chunks(w):
        w = np.asarray(w)
        return w.reshape(-1, P, w.shape[1]).transpose(1, 0, 2)

    def columns(b):
        return np.asarray(b).reshape(-1, P).T

    def head_groups(w):
        w = np.asarray(w)
        return w.reshape(*w.shape[:-1], GH, GROUPS, HD).swapaxes(-3, -2).swapaxes(-1, -2).reshape(
            *w.shape[:-1], GROUPS, P)

    xs, cs, wa, ba = (np.asarray(t) for t in (x, ctx_1024, L0_xattn_w_attn, L0_xattn_b_attn))
    w_qk = np.stack([head_groups(wa[:, :D]), head_groups(wa[:, D:2 * D])], 1)
    b_qk = np.stack([head_groups(ba[:D]), head_groups(ba[D:2 * D])], 0)
    arrays = {
        "x_tok": xs.reshape(B, TB, P, D).transpose(0, 2, 1, 3),
        "x_chan": xs.transpose(0, 2, 1).reshape(B, KC, P, S).transpose(0, 2, 1, 3),
        "ctx_tok": cs,
        "ctx_chan": cs.transpose(0, 2, 1).reshape(B, KC, P, SE).transpose(0, 2, 1, 3),
        "mask": np.asarray(mask_BxS2_ik0),
        "w_qk": w_qk.reshape(KC, P, 2, GROUPS, P).transpose(1, 0, 2, 3, 4),
        "b_qk": b_qk.transpose(2, 0, 1),
        "w_v": chunks(wa[:, 2 * D:]),
        "b_v": ba[2 * D:],
        "w_o": chunks(L0_xattn_w_oproj),
        "b_o": L0_xattn_b_oproj,
        "w_fc": chunks(L0_xattn_w_fc),
        "b_fc": columns(L0_xattn_b_fc),
        "w_m": chunks(L0_xattn_w_mproj),
        "b_m": L0_xattn_b_mproj,
        "g1": L0_xattn_ln1_g,
        "be1": L0_xattn_ln1_b,
        "g2": L0_xattn_ln2_g,
        "be2": L0_xattn_ln2_b,
        "w1T": chunks(np.asarray(L1_xattn_W1).T),
        "b1": columns(L1_xattn_b1),
        "w2T": chunks(np.asarray(L1_xattn_W2).T),
        "b2": L1_xattn_b2,
    }
    arrays = {f"in_{k}": np.ascontiguousarray(np.asarray(v)) for k, v in arrays.items()}
    nc = bacc.Bacc("TRN2", target_bir_lowering=False, num_devices=1)
    args = [nc.dram_tensor(k, v.shape, mybir.dt.from_np(v.dtype), kind="ExternalInput").ap() for k, v in arrays.items()]
    args.append(nc.dram_tensor("out_0", (B, P, TB, D), F32, kind="ExternalOutput").ap())
    build(nc, *args)
    got = run_bass_kernel_spmd(nc, [arrays], core_ids=[0]).results[0]["out_0"]
    return np.ascontiguousarray(got.transpose(0, 2, 1, 3).reshape(B, S, D))
```
